# Optimizing a Trainium2 kernel written in Bass

```python
import numpy as np
import jax
import jax.numpy as jnp

def _softmax(x, axis=-1):
    return jax.nn.softmax(x, axis=axis)

def _gelu(x):
    return jax.nn.gelu(x, approximate=True)

def _silu(x):
    return jax.nn.silu(x)

def _sigmoid(x):
    return jax.nn.sigmoid(x)

def _layernorm(x, axis=-1, eps=1e-05):
    m = jnp.mean(x, axis=axis, keepdims=True)
    v = jnp.var(x, axis=axis, keepdims=True)
    return (x - m) / jnp.sqrt(v + eps)

def _scatter_add(tgt, idx, src, axis=0):
    return tgt.at[idx].add(src)

def _segment_sum(src, seg, n):
    return jax.ops.segment_sum(src, seg, n)
kernel_name = 'mk_adaln_ffn_d1_seqx_r8_3c47c7'

def setup_inputs(seed: int=0):
    np.random.seed(seed)
    _w = jnp.asarray

    def _rec_inputs():
        import jax
        import jax.numpy as jnp
        _rk = jax.random.key(seed)
        x = -0.0002928 + 1 * jax.random.normal(jax.random.fold_in(_rk, 1), (2, 512, 128), jnp.float32)
        _lenS = 512 - jax.random.randint(jax.random.fold_in(_rk, 7), (2,), 0, max(1, 512 // 4) + 1, jnp.int32)
        _lenS2 = 512 - jax.random.randint(jax.random.fold_in(_rk, 8), (2,), 0, max(1, 512 // 4) + 1, jnp.int32)
        cond_256 = -0.106481 + 1.03144 * jax.random.normal(jax.random.fold_in(_rk, 11), (2, 32), jnp.float32)
        return (x, cond_256)
    x, cond_256 = _rec_inputs()

    def _L0_cond_setup():
        import jax, jax.numpy as jnp
        import numpy as np
        TOP_K = 2
        EPS = 1e-06
        B, S, H, G, E, M = (2, 256, 128, 32, 8, 256)
        key = jax.random.key(seed)
        ks = jax.random.split(key, 16)
        s_h = 1.0 / np.sqrt(H)
        s_g = 1.0 / np.sqrt(G)
        s_m = 1.0 / np.sqrt(M)
        return {'x': jax.random.normal(ks[0], (B, S, H), jnp.float32), 'genre_embed': jax.random.normal(ks[1], (B, 1, G), jnp.float32), 'rms_w': jnp.ones((H,), jnp.float32), 'wg_W': jax.random.normal(ks[2], (H, E), jnp.float32) * s_h, 'wg_b': jnp.zeros((E,), jnp.float32), 'gg_W': jax.random.normal(ks[3], (G, E), jnp.float32) * s_g, 'gg_b': jnp.zeros((E,), jnp.float32), 'W1': jax.random.normal(ks[4], (E, H, M), jnp.float32) * s_h, 'b1': jnp.zeros((E, M), jnp.float32), 'W2': jax.random.normal(ks[5], (E, M, M), jnp.float32) * s_m, 'b2': jnp.zeros((E, M), jnp.float32), 'W3': jax.random.normal(ks[6], (E, M, H), jnp.float32) * s_m, 'b3': jnp.zeros((E, H), jnp.float32)}
    _L0_cond_all = _L0_cond_setup()
    _L0_cond_in = {k: v for k, v in _L0_cond_all.items() if k in ('rms_w', 'wg_W', 'wg_b', 'gg_W', 'gg_b', 'W1', 'b1', 'W2', 'b2', 'W3', 'b3')}
    del _L0_cond_all

    def _L0_ffn_setup():
        import jax, jax.numpy as jnp
        import numpy as np
        FEATURES = 128
        D_IN = 128

        def fp8_gemm_optimized(x, input_scale, kernel, kernel_scale):
            s_in = input_scale[0]
            s_k = kernel_scale[0]
            x_q = (x.astype(jnp.float32) / s_in).astype(jnp.float8_e4m3fn)
            k_q = (kernel.astype(jnp.float32) / s_k).astype(jnp.float8_e4m3fn)
            y = jnp.dot(x_q.astype(jnp.float32), k_q.astype(jnp.float32), preferred_element_type=jnp.float32)
            return y * (s_in * s_k)
        key = jax.random.key(seed)
        kx, kk, kb = jax.random.split(key, 3)
        x = jax.random.normal(kx, (4, 1024, D_IN), dtype=jnp.float32)
        limit = np.sqrt(6.0 / (D_IN + FEATURES)).astype(np.float32)
        kernel = jax.random.uniform(kk, (D_IN, FEATURES), dtype=jnp.float32, minval=-limit, maxval=limit).astype(jnp.bfloat16)
        input_scale = jnp.ones((1,), dtype=jnp.float32)
        kernel_scale = jnp.ones((1,), dtype=jnp.float32)
        bias = jnp.zeros((FEATURES,), dtype=jnp.bfloat16)
        return {'x': x, 'kernel': kernel, 'input_scale': input_scale, 'kernel_scale': kernel_scale, 'bias': bias}
    _L0_ffn_all = _L0_ffn_setup()
    _L0_ffn_in = {k: v for k, v in _L0_ffn_all.items() if k in ('kernel', 'input_scale', 'kernel_scale', 'bias')}
    del _L0_ffn_all
    return {'x': x, 'cond_256': cond_256, 'L0_cond_rms_w': _L0_cond_in['rms_w'], 'L0_cond_wg_W': _L0_cond_in['wg_W'], 'L0_cond_wg_b': _L0_cond_in['wg_b'], 'L0_cond_gg_W': _L0_cond_in['gg_W'], 'L0_cond_gg_b': _L0_cond_in['gg_b'], 'L0_cond_W1': _L0_cond_in['W1'], 'L0_cond_b1': _L0_cond_in['b1'], 'L0_cond_W2': _L0_cond_in['W2'], 'L0_cond_b2': _L0_cond_in['b2'], 'L0_cond_W3': _L0_cond_in['W3'], 'L0_cond_b3': _L0_cond_in['b3'], 'L0_ffn_kernel': _L0_ffn_in['kernel'], 'L0_ffn_input_scale': _L0_ffn_in['input_scale'], 'L0_ffn_kernel_scale': _L0_ffn_in['kernel_scale'], 'L0_ffn_bias': _L0_ffn_in['bias']}

def reference(x, cond_256, L0_cond_rms_w, L0_cond_wg_W, L0_cond_wg_b, L0_cond_gg_W, L0_cond_gg_b, L0_cond_W1, L0_cond_b1, L0_cond_W2, L0_cond_b2, L0_cond_W3, L0_cond_b3, L0_ffn_kernel, L0_ffn_input_scale, L0_ffn_kernel_scale, L0_ffn_bias):
    import jax
    import jax.numpy as jnp

    def _L0_cond_ref(x, genre_embed, rms_w, wg_W, wg_b, gg_W, gg_b, W1, b1, W2, b2, W3, b3):
        import jax, jax.numpy as jnp
        import numpy as np
        TOP_K = 2
        EPS = 1e-06
        E = W1.shape[0]
        var = jnp.mean(x * x, axis=-1, keepdims=True)
        xn = rms_w * (x * jax.lax.rsqrt(var + EPS))
        gate = xn @ wg_W + wg_b + (genre_embed @ gg_W + gg_b)
        gate_w = jax.nn.softmax(gate, axis=-1)
        topk_w, topk_i = jax.lax.top_k(gate_w, TOP_K)
        cw = jnp.sum(jax.nn.one_hot(topk_i, E, dtype=x.dtype) * topk_w[..., None], axis=-2)
        h1 = jax.nn.relu(jnp.einsum('bsh,ehm->bsem', x, W1) + b1)
        h2 = jax.nn.relu(jnp.einsum('bsem,emn->bsen', h1, W2) + b2)
        out_e = jnp.einsum('bsen,enh->bseh', h2, W3) + b3
        return jnp.einsum('bseh,bse->bsh', out_e, cw)

    def _L0_ffn_ref(x, kernel, input_scale, kernel_scale, bias):
        import jax, jax.numpy as jnp
        import numpy as np
        FEATURES = 128
        D_IN = 128

        def fp8_gemm_optimized(x, input_scale, kernel, kernel_scale):
            s_in = input_scale[0]
            s_k = kernel_scale[0]
            x_q = (x.astype(jnp.float32) / s_in).astype(jnp.float8_e4m3fn)
            k_q = (kernel.astype(jnp.float32) / s_k).astype(jnp.float8_e4m3fn)
            y = jnp.dot(x_q.astype(jnp.float32), k_q.astype(jnp.float32), preferred_element_type=jnp.float32)
            return y * (s_in * s_k)
        dtype = jnp.bfloat16
        x = x.astype(dtype)
        orig_shape = x.shape
        x2 = x.reshape(-1, x.shape[-1])
        y = fp8_gemm_optimized(x2, input_scale, kernel, kernel_scale)
        y = y.astype(dtype) + bias
        return y.reshape(orig_shape[:-1] + (FEATURES,))
    x = x + _L0_ffn_ref(_L0_cond_ref(x, cond_256[:, None, :], L0_cond_rms_w, L0_cond_wg_W, L0_cond_wg_b, L0_cond_gg_W, L0_cond_gg_b, L0_cond_W1, L0_cond_b1, L0_cond_W2, L0_cond_b2, L0_cond_W3, L0_cond_b3), L0_ffn_kernel, L0_ffn_input_scale, L0_ffn_kernel_scale, L0_ffn_bias)
    return x

_drawn_inputs = setup_inputs


def setup_inputs(seed=0):
    import zlib

    import numpy as np

    out = dict(_drawn_inputs(seed))
    spreads = {'L0_cond_rms_w': (1.0, 0.2),
     'L0_cond_wg_b': (0.0, 0.1),
     'L0_cond_gg_b': (0.0, 0.1),
     'L0_cond_b1': (0.0, 0.323),
     'L0_cond_b2': (0.0, 0.1),
     'L0_cond_b3': (0.0, 0.1),
     'L0_ffn_bias': (0.0, 0.1)}
    factors = {}
    for name, (base, spread) in spreads.items():
        noise = np.random.default_rng([zlib.crc32(name.encode()), seed]).standard_normal(out[name].shape)
        drawn = base * np.exp(spread * noise) if base else spread * noise
        out[name] = jnp.asarray(drawn.astype(out[name].dtype))
    for name, factor in factors.items():
        out[name] = (out[name] * factor).astype(out[name].dtype)
    return out
```

```python
from contextlib import ExitStack

import concourse.bass as bass
from concourse import mybir
from concourse.alu_op_type import AluOpType as ALU

ACT = mybir.ActivationFunctionType
AX = mybir.AxisListType
F32 = mybir.dt.float32
F32R = mybir.dt.float32r
BF16 = mybir.dt.bfloat16
I32 = mybir.dt.int32

P = 128
EPS = 1e-6
EXPONENT_BITS = 0x7F800000
F8_LEAST_NORMAL = 2.0 ** -6
F8_ROUNDER = 1.5 * 2.0 ** 20
F8_OVERFLOW = 7.3e35


def adaln_ffn(nc, x, cond, rms_w, wg_W, wg_b, gg_W, gg_b, W1, b1, W2, b2, W3, b3,
              ffn_kernel, input_scale, kernel_scale, ffn_bias, out):
    B, S, H = x.shape
    E, _, M = W1.shape
    G = gg_W.shape[0]
    T = B * S // P
    HT = T // 2
    N = HT * P
    MT = M // P
    U = 2 * E
    PB = P // B
    assert (H, B, MT, N, G, E) == (P, 2, 2, 512, 32, 8)
    LOOP_FROM, LOOP_TURNS = 2, 3
    LOOP_END = LOOP_FROM + 4 * LOOP_TURNS

    x_tokens = x.rearrange("b (q t) h -> (b q) t h", t=T)
    out_tokens = out.rearrange("b (q t) h -> (b q) t h", t=T)

    def steps(engine, first, last, body):
        for s in range(first, LOOP_FROM):
            body(s, s % 4)
        with engine.Fori(0, LOOP_TURNS) as i:
            for j in range(4):
                body(LOOP_FROM + j + i * 4, (LOOP_FROM + j) % 4)
        for s in range(LOOP_END, last + 1):
            body(s, s % 4)

    def wait(engine, sem, value):
        if not isinstance(value, int) or value > 0:
            engine.wait_ge(sem, value)

    with ExitStack() as ctx:
        def sb(name, shape, dt):
            return ctx.enter_context(nc.sbuf_tensor(name, shape, dt))

        def sem(name):
            return ctx.enter_context(nc.semaphore(name))

        x_tok = sb("x_tok", [P, T, H], F32)
        x_hi = sb("x_hi", [P, 2, N], F32R)
        x_lo = sb("x_lo", [P, 2, N], F32R)
        ident = sb("ident", [P, P], F32)
        w_raw = [sb("w1_raw", [P, 2, 1, M], F32), sb("w2_raw", [P, 2, MT, M], F32), sb("w3_raw", [P, 2, MT, H], F32)]
        w_hi = [sb("w1_hi", [P, 2, 1, M], F32R), sb("w2_hi", [P, 2, MT, M], F32R), sb("w3_hi", [P, 2, MT, H], F32R)]
        w_lo = [sb("w1_lo", [P, 2, 1, M], F32R), sb("w2_lo", [P, 2, MT, M], F32R), sb("w3_lo", [P, 2, MT, H], F32R)]
        bias_rows = sb("bias_rows", [2 * E * MT, P], F32)
        bias_cols = sb("bias_cols", [P, 2, E, MT], F32)
        bias_slot = sb("bias_slot", [P, 2, 2, MT], F32)
        b3_sb = sb("b3_sb", [E, H], F32)
        h1 = sb("h1", [P, 2, MT, N], F32)
        h1_hi = sb("h1_hi", [P, 2, MT, N], F32R)
        h1_lo = sb("h1_lo", [P, 2, MT, N], F32R)
        h2 = sb("h2", [P, 2, MT, N], F32)
        h2_cw = sb("h2_cw", [P, 2, MT, N], F32)
        h2_hi = sb("h2_hi", [P, 2, MT, N], F32R)
        h2_lo = sb("h2_lo", [P, 2, MT, N], F32R)
        x_sq = sb("x_sq", [P, T, H], F32)
        sum_sq = sb("sum_sq", [P, T], F32)
        var_eps = sb("var_eps", [P, T], F32)
        minus_half = sb("minus_half", [P, T], F32)
        inv_rms = sb("inv_rms", [P, T], F32)
        rms_col = sb("rms_col", [P, 1], F32)
        wg_raw = sb("wg_raw", [P, E], F32)
        wg_scaled = sb("wg_scaled", [P, E], F32)
        wg_hi = sb("wg_hi", [P, E], F32R)
        wg_lo = sb("wg_lo", [P, E], F32R)
        condT = sb("condT", [G, B], F32)
        genre_lhs = sb("genre_lhs", [G + 2, P], F32)
        genre_rhs = sb("genre_rhs", [G + 2, E], F32)
        gate_bias = sb("gate_bias", [P, E], F32)
        order = sb("order", [P, T, E], F32)
        logits = sb("logits", [P, T, E], F32)
        shifted = sb("shifted", [P, T, E], F32)
        top = sb("top", [P, T], F32)
        prob = sb("prob", [P, T, E], F32)
        prob_sum = sb("prob_sum", [P, T], F32)
        prob_inv = sb("prob_inv", [P, T], F32)
        best = sb("best", [P, T], F32)
        ties = sb("ties", [P, T, E], F32)
        first_of = sb("first_of", [P, T], F32)
        chosen1 = sb("chosen1", [P, T, E], F32)
        chosen2 = sb("chosen2", [P, T, E], F32)
        rest = sb("rest", [P, T, E], F32)
        cw = sb("cw", [P, T, E], F32)
        cw_T = sb("cw_T", [E, T * P], F32)
        cw_row = sb("cw_row", [1, E, T * P], F32)
        cw_bc = sb("cw_bc", [P, E, T * P], F32)
        s_in = sb("s_in", [P, 1], F32)
        s_k = sb("s_k", [P, 1], F32)
        s_hi = sb("s_hi", [P, 2], F32R)
        s_lo = sb("s_lo", [P, 2], F32)
        s_inv = sb("s_inv", [P, 2], F32)
        s_inv_neg = sb("s_inv_neg", [P, 2], F32)
        s_both = sb("s_both", [P, 1], F32)
        k_raw = sb("k_raw", [P, H], BF16)
        k_q = sb("k_q", [P, H], BF16)
        bias_bc = sb("bias_bc", [P, H], BF16)
        cond_out = sb("cond_out", [P, 2, N], BF16)
        cond_q = sb("cond_q", [P, 2, N], BF16)
        q_t = sb("q_t", [P, N], BF16)
        q_e = sb("q_e", [P, N], F32)
        q_e2 = sb("q_e2", [P, N], F32)
        q_v = sb("q_v", [P, N], F32)
        q_m = sb("q_m", [P, N], I32)
        q_r = sb("q_r", [P, N], F32)
        q_s = sb("q_s", [P, N], F32)
        q_f = sb("q_f", [P, N], BF16)
        q_nan = sb("q_nan", [P, N], BF16)
        y_bf = sb("y_bf", [P, 2, N], BF16)
        y_biased = sb("y_biased", [P, 2, N], BF16)
        y_out = sb("y_out", [P, 2, N], F32)

        def bank(name):
            return ctx.enter_context(nc.psum_tensor(name, [P, N], F32))

        acc = [bank("acc0"), bank("acc1")]
        z1 = [bank("z1_0"), bank("z1_1")]
        z2 = [bank("z2_0"), bank("z2_1")]
        misc = [bank("misc0"), bank("misc1")]

        x_loaded = [sem("x_loaded0"), sem("x_loaded1")]
        w_loaded = [[sem(f"w{l + 1}_loaded{p}") for p in range(2)] for l in range(3)]
        gate_w_loaded = sem("gate_w_loaded")
        genre_loaded = sem("genre_loaded")
        bias_loaded = sem("bias_loaded")
        b3_loaded = sem("b3_loaded")
        ffn_loaded = sem("ffn_loaded")
        ffn_bias_loaded = sem("ffn_bias_loaded")
        zeroed = sem("zeroed")
        ident_ready = sem("ident_ready")
        consts_ready = sem("consts_ready")
        genre_lhs_ready = sem("genre_lhs_ready")
        xT_ready = sem("xT_ready")
        x_hi_ready = sem("x_hi_ready")
        x_lo_ready = sem("x_lo_ready")
        x_sq_ready = sem("x_sq_ready")
        var_ready = sem("var_ready")
        inv_rms_ready = sem("inv_rms_ready")
        wg_split = sem("wg_split")
        gate_bias_ps = sem("gate_bias_ps")
        bias_cols_ps = sem("bias_cols_ps")
        logits_ps = sem("logits_ps")
        shifted_ready = sem("shifted_ready")
        prob_ready = sem("prob_ready")
        cw_ready = sem("cw_ready")
        cwT_ps = sem("cwT_ps")
        cwT_ready = sem("cwT_ready")
        cw_row_loaded = sem("cw_row_loaded")
        cw_bc_ready = sem("cw_bc_ready")
        w_hi_ready = [sem(f"w{l + 1}_hi_ready") for l in range(3)]
        w_lo_ready = [sem(f"w{l + 1}_lo_ready") for l in range(3)]
        bias_slot_ready = sem("bias_slot_ready")
        z1_ready = sem("z1_ready")
        z2_ready = sem("z2_ready")
        acc_added = sem("acc_added")
        h1_ready = sem("h1_ready")
        h1_hi_ready = sem("h1_hi_ready")
        h1_lo_ready = sem("h1_lo_ready")
        h2_ready = sem("h2_ready")
        h2_scaled = sem("h2_scaled")
        h2_hi_ready = sem("h2_hi_ready")
        h2_lo_ready = sem("h2_lo_ready")
        dve_chain = sem("dve_chain")
        k_q_ready = sem("k_q_ready")
        cond_out_ready = sem("cond_out_ready")
        cond_q_ready = sem("cond_q_ready")
        y_ps = sem("y_ps")
        y_bf_ready = sem("y_bf_ready")
        y_out_ready = sem("y_out_ready")
        stored = sem("stored")

        block = ctx.enter_context(nc.Block())

        @block.sync
        def _(sp):
            def load_weights(l, expert, slot):
                W = (W1, W2, W3)[l]
                src = W[bass.ds(expert, 1), :, :] if not isinstance(expert, int) else W[expert:expert + 1, :, :]
                sp.dma_start(w_raw[l][:, slot, :, :], src.rearrange("e (k p) n -> p (e k) n", p=P))\
                    .then_inc(w_loaded[l][slot], 16)

            sp.dma_start(x_tok[:, 0:HT, :], x_tokens[:, 0:HT, :]).then_inc(x_loaded[0], 16)
            load_weights(0, 0, 0)
            sp.dma_start(x_tok[:, HT:T, :], x_tokens[:, HT:T, :]).then_inc(x_loaded[1], 16)
            load_weights(1, 0, 0)
            load_weights(2, 0, 0)
            for l in range(3):
                load_weights(l, 1, 1)
            sp.wait_ge(cwT_ready, 2)
            sp.dma_start(cw_row[0:1, :, :], cw_T[:, :]).then_inc(cw_row_loaded, 16)
            with sp.Fori(0, (E - 2) // 2) as i:
                for slot in range(2):
                    for l in range(3):
                        sp.wait_ge(w_lo_ready[l], i * 2 + (slot + 1))
                        load_weights(l, i * 2 + (2 + slot), slot)
            for h in range(2):
                sp.wait_ge(y_out_ready, h + 1)
                sp.dma_start(out_tokens[:, h * HT:(h + 1) * HT, :],
                             y_out[:, h, :].rearrange("p (t f) -> p t f", f=H)).then_inc(stored, 16)
            sp.wait_ge(stored, 32)

        @block.gpsimd
        def _(pool):
            pool.memset(ident[:, :], 0.0).then_inc(zeroed, 1)
            pool.wait_ge(zeroed, 1)
            pool.affine_select(out=ident[:, :], in_=ident[:, :], compare_op=ALU.not_equal, fill=1.0, base=0,
                               pattern=[[-1, P]], channel_multiplier=1).then_inc(ident_ready, 1)
            pool.memset(genre_lhs[:, :], 1.0).then_inc(consts_ready, 1)
            pool.memset(minus_half[:, :], -0.5).then_inc(consts_ready, 1)
            for e in range(E):
                pool.memset(order[:, :, e:e + 1], float(E - e)).then_inc(consts_ready, 1)

            def low_part(l, expert, slot):
                pool.wait_ge(w_hi_ready[l], expert + 1)
                pool.tensor_tensor(w_lo[l][:, slot, :, :], w_raw[l][:, slot, :, :],
                                   w_hi[l][:, slot, :, :].bitcast(F32), ALU.subtract).then_inc(w_lo_ready[l], 1)

            low_part(0, 0, 0)
            for h in range(2):
                pool.wait_ge(x_loaded[h], 16)
                part = x_tok[:, h * HT:(h + 1) * HT, :]
                pool.tensor_tensor(x_sq[:, h * HT:(h + 1) * HT, :], part, part, ALU.mult).then_inc(x_sq_ready, 1)
            low_part(1, 0, 0)
            pool.wait_ge(consts_ready, 2)
            pool.wait_ge(var_ready, 1)
            pool.tensor_tensor(inv_rms[:, :], var_eps[:, :], minus_half[:, :], ALU.pow).then_inc(inv_rms_ready, 1)

            def step(r, k):
                if r % 2 == 0:
                    for l in range(2):
                        low_part(l, k + 1, 1 - r // 2)
                else:
                    low_part(2, k, r // 2)

            step(0, 0)
            step(1, 0)
            pool.wait_ge(cw_row_loaded, 16)
            for e in range(E):
                pool.partition_broadcast(cw_bc[:, e, :], cw_row[0:1, e, :], P).then_inc(cw_bc_ready, 1)
            with pool.Fori(0, LOOP_TURNS) as i:
                for j in range(4):
                    step((LOOP_FROM + j) % 4, i * 2 + (LOOP_FROM + j) // 2)
            low_part(2, E - 1, (E - 1) % 2)

        @block.scalar
        def _(act):
            act.dma_start(wg_raw[:, :], wg_W).then_inc(gate_w_loaded, 16)
            act.dma_start(rms_col[:, :], rms_w.rearrange("(p o) -> p o", o=1)).then_inc(gate_w_loaded, 16)
            act.dma_start(bias_rows[0:E * MT, :], b1.rearrange("e (m p) -> (e m) p", p=P)).then_inc(bias_loaded, 16)
            act.dma_start(bias_rows[E * MT:2 * E * MT, :], b2.rearrange("e (m p) -> (e m) p", p=P)).then_inc(bias_loaded, 16)
            act.dma_start(condT[:, :], cond.rearrange("b g -> g b"), allow_slow_non_contiguous=True).then_inc(genre_loaded, 16)
            act.dma_start(genre_rhs[0:G, :], gg_W).then_inc(genre_loaded, 16)
            act.dma_start(genre_rhs[G:G + 1, :], wg_b.rearrange("(o e) -> o e", o=1)).then_inc(genre_loaded, 16)
            act.dma_start(genre_rhs[G + 1:G + 2, :], gg_b.rearrange("(o e) -> o e", o=1)).then_inc(genre_loaded, 16)
            act.dma_start(b3_sb[:, :], b3).then_inc(b3_loaded, 16)
            act.dma_start(k_raw[:, :], ffn_kernel).then_inc(ffn_loaded, 16)
            act.dma_start(s_in[:, :], input_scale.partition_broadcast(P)).then_inc(ffn_loaded, 16)
            act.dma_start(s_k[:, :], kernel_scale.partition_broadcast(P)).then_inc(ffn_loaded, 16)
            act.dma_start(bias_bc[:, :], ffn_bias.partition_broadcast(P)).then_inc(ffn_bias_loaded, 16)

            def high_part(l, expert, expert_div, slot):
                act.wait_ge(w_loaded[l][slot], (expert_div + 1) * 16)
                if not isinstance(expert, int) or expert >= 2:
                    used, per_expert, before = ((z1_ready, 2 * MT, 0), (z2_ready, 2 * MT, 0), (acc_added, 2, 2))[l]
                    act.wait_ge(used, (expert - 1) * per_expert + before)
                act.activation(w_hi[l][:, slot, :, :], w_raw[l][:, slot, :, :], ACT.Copy).then_inc(w_hi_ready[l], 1)

            def relu(z, ready, layer, m, u, r, to, done):
                act.wait_ge(ready, u * 2 + (m + 1))
                act.activation(to[:, r % 2, m, :], z[m][:, :], ACT.Relu,
                               bias=bias_slot[:, r // 2, layer, m:m + 1]).then_inc(done, 1)

            def step(s, r, layer1=True, layer2=True, k=None):
                if layer1:
                    u, ur = s + 1, (r + 1) % 4
                    act.wait_ge(bias_slot_ready, k1(u, k, r))
                    wait(act, h1_lo_ready, u - 1)
                    for m in range(MT):
                        relu(z1, z1_ready, 0, m, u, ur, h1, h1_ready)
                    act.wait_ge(h1_ready, u * 2 + 2)
                    wait(act, z2_ready, u * 2 - 2)
                    act.activation(h1_hi[:, ur % 2, :, :], h1[:, ur % 2, :, :], ACT.Copy).then_inc(h1_hi_ready, 1)
                if layer2:
                    wait(act, h2_scaled, s - 1)
                    for m in range(MT):
                        relu(z2, z2_ready, 1, m, s, r, h2, h2_ready)

            def k1(u, k, r):
                return k + 1 if r % 2 == 0 else k + 2

            def weights_due(r, k):
                if r % 2 == 0:
                    for l in range(2):
                        high_part(l, k + 1, due_div(k, r, 1), 1 - r // 2)
                else:
                    high_part(2, k, due_div(k, r, 0), r // 2)

            def due_div(k, r, ahead):
                if isinstance(k, int):
                    return (k + ahead) // 2
                return k_half[0] + (r // 2 + ahead) // 2

            k_half = [0]

            high_part(0, 0, 0, 0)
            for h in range(2):
                act.wait_ge(xT_ready, h + 1)
                act.activation(x_hi[:, h, :], misc[h][:, :], ACT.Copy).then_inc(x_hi_ready, 1)
            high_part(1, 0, 0, 0)
            act.wait_ge(bias_slot_ready, 1)
            for m in range(MT):
                relu(z1, z1_ready, 0, m, 0, 0, h1, h1_ready)
            act.wait_ge(h1_ready, 2)
            act.activation(h1_hi[:, 0, :, :], h1[:, 0, :, :], ACT.Copy).then_inc(h1_hi_ready, 1)
            act.wait_ge(shifted_ready, 1)
            act.activation(prob[:, :, :], shifted[:, :, :], ACT.Exp).then_inc(prob_ready, 1)
            for s in range(2):
                step(s, s, k=0)
                weights_due(s, 0)
            with act.Fori(0, LOOP_TURNS) as i:
                for j in range(4):
                    s = LOOP_FROM + j
                    k = i * 2 + s // 2
                    k_half[0] = i + s // 4
                    step(i * 4 + s, s % 4, k=k)
                    weights_due(s % 4, k)
            step(U - 2, (U - 2) % 4, k=E - 1)
            high_part(2, E - 1, (E - 1) // 2, (E - 1) % 2)
            step(U - 1, (U - 1) % 4, layer1=False, k=E - 1)

            for h in range(2):
                act.wait_ge(acc_added, U + 1 + h)
                act.activation(cond_out[:, h, :], acc[h][:, :], ACT.Copy).then_inc(cond_out_ready, 1)
            for h in range(2):
                act.wait_ge(y_ps, h + 1)
                act.activation(y_bf[:, h, :], misc[h][:, :], ACT.Copy, scale=s_both[:, 0:1]).then_inc(y_bf_ready, 1)

        @block.vector
        def _(dve):
            count = [0]

            def link(instruction):
                count[0] += 1
                instruction.then_inc(dve_chain, 1)
                dve.wait_ge(dve_chain, count[0])

            def per_token(v):
                return v[:, :].unsqueeze(2).to_broadcast([P, T, E])

            def quantise(src, dst, scale, w, done):
                t, e, e2, v, m, rr, sm, f, nan = (a[:, 0:w] for a in (q_t, q_e, q_e2, q_v, q_m, q_r, q_s, q_f, q_nan))
                c = slice(scale, scale + 1)
                link(dve.tensor_scalar(t, src, s_inv[:, c], None, ALU.mult))
                link(dve.scalar_tensor_tensor(e, t, s_hi[:, c].bitcast(F32), src, ALU.mult, ALU.subtract))
                link(dve.scalar_tensor_tensor(e2, t, s_lo[:, c], e, ALU.mult, ALU.add))
                link(dve.scalar_tensor_tensor(v, e2, s_inv_neg[:, c], t, ALU.mult, ALU.add))
                link(dve.tensor_scalar(m, v.bitcast(I32), EXPONENT_BITS, None, ALU.bitwise_and))
                link(dve.tensor_scalar(rr, m.bitcast(F32), F8_LEAST_NORMAL, F8_ROUNDER, ALU.max, ALU.mult))
                link(dve.tensor_tensor(sm, v, rr, ALU.add))
                link(dve.tensor_tensor(f, sm, rr, ALU.subtract))
                link(dve.tensor_scalar(nan, f, F8_OVERFLOW, 0.0, ALU.mult, ALU.mult))
                dve.tensor_tensor(dst, f, nan, ALU.add).then_inc(done, 1)

            dve.wait_ge(gate_w_loaded, 32)
            link(dve.tensor_scalar(wg_scaled[:, :], wg_raw[:, :], rms_col[:, 0:1], None, ALU.mult))
            link(dve.tensor_copy(wg_hi[:, :], wg_scaled[:, :]))
            dve.tensor_tensor(wg_lo[:, :], wg_scaled[:, :], wg_hi[:, :].bitcast(F32), ALU.subtract).then_inc(wg_split, 1)
            for h in range(2):
                dve.wait_ge(x_hi_ready, h + 1)
                dve.tensor_tensor(x_lo[:, h, :], misc[h][:, :], x_hi[:, h, :].bitcast(F32), ALU.subtract)\
                    .then_inc(x_lo_ready, 1)
            dve.wait_ge(x_sq_ready, 2)
            link(dve.reduce_sum(sum_sq[:, :], x_sq[:, :, :], AX.X))
            dve.tensor_scalar(var_eps[:, :], sum_sq[:, :], 1.0 / H, EPS, ALU.mult, ALU.add).then_inc(var_ready, 1)
            dve.wait_ge(consts_ready, 2)
            dve.wait_ge(genre_loaded, 64)
            for b in range(B):
                dve.tensor_copy(genre_lhs[0:G, b * PB:(b + 1) * PB], condT[:, b:b + 1].to_broadcast([G, PB]))\
                    .then_inc(genre_lhs_ready, 1)
            dve.wait_ge(bias_cols_ps, 1)
            link(dve.tensor_copy(bias_cols[:, :, :, :].rearrange("p l e m -> p (l e m)"), z2[0][:, 0:2 * E * MT]))

            def load_bias_slot(expert, slot):
                src = bias_cols[:, :, bass.ds(expert, 1), :] if not isinstance(expert, int) else bias_cols[:, :, expert:expert + 1, :]
                dve.tensor_scalar(bias_slot[:, slot, :, :], src.rearrange("p l o m -> p l (o m)"), 1.0, None, ALU.mult)\
                    .then_inc(bias_slot_ready, 1)

            load_bias_slot(0, 0)
            dve.wait_ge(gate_bias_ps, 1)
            link(dve.tensor_copy(gate_bias[:, :], z2[1][:, 0:E]))
            dve.wait_ge(inv_rms_ready, 1)
            dve.wait_ge(logits_ps, 1)
            link(dve.tensor_tensor(logits[:, :, :], acc[0][:, 0:T * E].rearrange("p (t e) -> p t e", e=E),
                                   per_token(inv_rms), ALU.mult))
            link(dve.tensor_tensor(logits[:, :, :], logits[:, :, :],
                                   gate_bias[:, :].unsqueeze(1).to_broadcast([P, T, E]), ALU.add))
            link(dve.reduce_max(top[:, :], logits[:, :, :], AX.X))
            dve.tensor_tensor(shifted[:, :, :], logits[:, :, :], per_token(top), ALU.subtract).then_inc(shifted_ready, 1)

            def h1_low(u, half):
                dve.wait_ge(h1_hi_ready, u + 1)
                dve.tensor_tensor(h1_lo[:, half, :, :], h1[:, half, :, :], h1_hi[:, half, :, :].bitcast(F32),
                                  ALU.subtract).then_inc(h1_lo_ready, 1)

            h1_low(0, 0)
            dve.wait_ge(prob_ready, 1)
            dve.wait_ge(consts_ready, 2 + E)
            link(dve.reduce_sum(prob_sum[:, :], prob[:, :, :], AX.X))
            link(dve.reciprocal(prob_inv[:, :], prob_sum[:, :]))

            def choose(of, chosen):
                link(dve.reduce_max(best[:, :], of[:, :, :], AX.X))
                link(dve.tensor_tensor(ties[:, :, :], of[:, :, :], per_token(best), ALU.is_equal))
                link(dve.tensor_tensor(ties[:, :, :], ties[:, :, :], order[:, :, :], ALU.mult))
                link(dve.reduce_max(first_of[:, :], ties[:, :, :], AX.X))
                link(dve.tensor_tensor(chosen[:, :, :], ties[:, :, :], per_token(first_of), ALU.is_equal))

            choose(prob, chosen1)
            link(dve.scalar_tensor_tensor(rest[:, :, :], chosen1[:, :, :], -2.0, prob[:, :, :], ALU.mult, ALU.add))
            choose(rest, chosen2)
            link(dve.tensor_tensor(chosen1[:, :, :], chosen1[:, :, :], chosen2[:, :, :], ALU.add))
            link(dve.tensor_tensor(cw[:, :, :], prob[:, :, :], chosen1[:, :, :], ALU.mult))
            dve.tensor_tensor(cw[:, :, :], cw[:, :, :], per_token(prob_inv), ALU.mult).then_inc(cw_ready, 1)
            load_bias_slot(1, 1)
            h1_low(1, 1)
            for h in range(2):
                dve.wait_ge(cwT_ps, h + 1)
                dve.tensor_copy(cw_T[:, h * N:(h + 1) * N], misc[h][0:E, :]).then_inc(cwT_ready, 1)

            dve.wait_ge(ffn_loaded, 48)
            for c, s in enumerate((s_in, s_k)):
                dve.tensor_copy(s_hi[:, c:c + 1], s[:, :])
                link(dve.reciprocal(s_inv[:, c:c + 1], s[:, :]))
                dve.tensor_tensor(s_lo[:, c:c + 1], s[:, :], s_hi[:, c:c + 1].bitcast(F32), ALU.subtract)
                link(dve.tensor_scalar(s_inv_neg[:, c:c + 1], s_inv[:, c:c + 1], -1.0, None, ALU.mult))
            link(dve.tensor_tensor(s_both[:, :], s_in[:, :], s_k[:, :], ALU.mult))
            quantise(k_raw[:, :], k_q[:, :], 1, H, k_q_ready)

            def step(s, r, k, layer1=True, layer2=True):
                if layer1:
                    if r % 2 == 0:
                        wait(dve, h2_ready, k * 4)
                        load_bias_slot(k + 1, 1 - r // 2)
                    h1_low(s + 1, (r + 1) % 2)
                if layer2:
                    u, half = s - 1, (r + 1) % 2
                    dve.wait_ge(h2_ready, u * 2 + 2)
                    expert = k if r % 2 else k - 1
                    if isinstance(expert, int):
                        dve.wait_ge(cw_bc_ready, expert + 1)
                        mix = cw_bc[:, expert:expert + 1, half * N:(half + 1) * N]
                    else:
                        dve.wait_ge(cw_bc_ready, expert + 1)
                        mix = cw_bc[:, bass.ds(expert, 1), half * N:(half + 1) * N]
                    dve.tensor_tensor(h2_cw[:, half, :, :], h2[:, half, :, :], mix.to_broadcast([P, MT, N]),
                                      ALU.mult).then_inc(h2_scaled, 1)
                    dve.wait_ge(h2_scaled, u + 1)
                    if not isinstance(u, int) or u >= 2:
                        dve.wait_ge(acc_added, u + 1)
                    dve.tensor_copy(h2_hi[:, half, :, :], h2_cw[:, half, :, :]).then_inc(h2_hi_ready, 1)
                    dve.wait_ge(h2_hi_ready, u + 1)
                    dve.tensor_tensor(h2_lo[:, half, :, :], h2_cw[:, half, :, :], h2_hi[:, half, :, :].bitcast(F32),
                                      ALU.subtract).then_inc(h2_lo_ready, 1)

            step(1, 1, 0)
            with dve.Fori(0, LOOP_TURNS) as i:
                for j in range(4):
                    s = LOOP_FROM + j
                    step(i * 4 + s, s % 4, i * 2 + s // 2)
            h1_low(U - 1, 1)
            step(U - 2, (U - 2) % 4, E - 1, layer1=False)
            step(U - 1, (U - 1) % 4, E - 1, layer1=False)
            step(U, U % 4, E, layer1=False)

            for h in range(2):
                dve.wait_ge(cond_out_ready, h + 1)
                quantise(cond_out[:, h, :], cond_q[:, h, :], 0, N, cond_q_ready)
            dve.wait_ge(ffn_bias_loaded, 16)
            for h in range(2):
                dve.wait_ge(y_bf_ready, h + 1)
                link(dve.tensor_tensor(y_biased[:, h, :].rearrange("p (t f) -> p t f", f=H),
                                       y_bf[:, h, :].rearrange("p (t f) -> p t f", f=H),
                                       bias_bc[:, :].unsqueeze(1).to_broadcast([P, HT, H]), ALU.add))
                dve.tensor_tensor(y_out[:, h, :], y_biased[:, h, :],
                                  x_tok[:, h * HT:(h + 1) * HT, :].rearrange("p t f -> p (t f)"), ALU.add)\
                    .then_inc(y_out_ready, 1)

        @block.tensor
        def _(pe):
            pe.wait_ge(ident_ready, 1)
            for h in range(2):
                pe.wait_ge(x_loaded[h], 16)
                for c in range(HT):
                    last = pe.transpose(misc[h][:, c * P:(c + 1) * P], x_tok[:, h * HT + c, :], ident[:, :])
                last.then_inc(xT_ready, 1)
            pe.wait_ge(bias_loaded, 32)
            nb = 2 * E * MT
            pe.transpose(z2[0][:, 0:nb], bias_rows[:, :], ident[0:nb, 0:nb]).then_inc(bias_cols_ps, 1)
            pe.wait_ge(genre_lhs_ready, 2)
            pe.matmul(z2[1][:, 0:E], genre_lhs[:, :], genre_rhs[:, :], start=True, stop=True).then_inc(gate_bias_ps, 1)
            pe.wait_ge(wg_split, 1)
            pe.wait_ge(x_lo_ready, 2)
            for c in range(T):
                hi = x_hi[:, c // HT, (c % HT) * P:(c % HT + 1) * P]
                lo = x_lo[:, c // HT, (c % HT) * P:(c % HT + 1) * P]
                for n, (a, b) in enumerate(((hi, wg_hi), (hi, wg_lo), (lo, wg_hi))):
                    last = pe.matmul(acc[0][:, c * E:(c + 1) * E], a, b[:, :], start=n == 0, stop=n == 2)
            last.then_inc(logits_ps, 1)

            def products(bank, parts, start, stop):
                n, passes = 0, 3 * len(parts)
                for wh, wl, mh, ml in parts:
                    for a, b in ((wh, mh), (wh, ml), (wl, mh)):
                        last = pe.matmul(bank, a, b, start=start and n == 0, stop=stop and n == passes - 1)
                        n += 1
                return last

            def layer1(u, r, expert):
                slot, half = r // 2, r % 2
                if half == 0:
                    pe.wait_ge(w_lo_ready[0], expert + 1)
                for m in range(MT):
                    wait(pe, h1_ready, u * 2 + (m - 1))
                    cols = slice(m * P, (m + 1) * P)
                    products(z1[m][:, :], [(w_hi[0][:, slot, 0, cols], w_lo[0][:, slot, 0, cols],
                                            x_hi[:, half, :], x_lo[:, half, :])], True, True).then_inc(z1_ready, 1)

            def layer2(u, r, expert):
                slot, half = r // 2, r % 2
                if half == 0:
                    pe.wait_ge(w_lo_ready[1], expert + 1)
                pe.wait_ge(h1_lo_ready, u + 1)
                for m in range(MT):
                    wait(pe, h2_ready, u * 2 + (m - 1))
                    cols = slice(m * P, (m + 1) * P)
                    products(z2[m][:, :], [(w_hi[1][:, slot, k, cols], w_lo[1][:, slot, k, cols],
                                            h1_hi[:, half, k, :], h1_lo[:, half, k, :]) for k in range(MT)],
                             True, True).then_inc(z2_ready, 1)

            def layer3(u, r, expert, stop=False):
                slot, half = r // 2, r % 2
                if half == 0:
                    pe.wait_ge(w_lo_ready[2], expert + 1)
                pe.wait_ge(h2_lo_ready, u + 1)
                products(acc[half][:, :], [(w_hi[2][:, slot, k, :], w_lo[2][:, slot, k, :],
                                            h2_hi[:, half, k, :], h2_lo[:, half, k, :]) for k in range(MT)],
                         False, stop).then_inc(acc_added, 1)

            pe.wait_ge(x_lo_ready, 1)
            layer1(0, 0, 0)
            layer1(1, 1, 0)
            pe.wait_ge(bias_slot_ready, 1)
            layer2(0, 0, 0)
            pe.wait_ge(cw_ready, 1)
            for h in range(2):
                for c in range(HT):
                    last = pe.transpose(misc[h][0:E, c * P:(c + 1) * P], cw[:, h * HT + c, :], ident[:, :])
                last.then_inc(cwT_ps, 1)
            layer1(2, 2, 1)
            layer2(1, 1, 0)
            pe.wait_ge(b3_loaded, 16)
            for h in range(2):
                pe.wait_ge(cwT_ready, h + 1)
                pe.matmul(acc[h][:, :], b3_sb[:, :], cw_T[:, h * N:(h + 1) * N], start=True, stop=False)\
                    .then_inc(acc_added, 1)
            with pe.Fori(0, LOOP_TURNS) as i:
                for j in range(4):
                    s = LOOP_FROM + j
                    layer1(i * 4 + (s + 1), (s + 1) % 4, i * 2 + (s + 1) // 2)
                    layer2(i * 4 + s, s % 4, i * 2 + s // 2)
                    layer3(i * 4 + (s - 2), (s - 2) % 4, i * 2 + (s - 2) // 2)
            layer1(U - 1, (U - 1) % 4, E - 1)
            layer2(U - 2, (U - 2) % 4, E - 1)
            layer3(U - 4, (U - 4) % 4, E - 2)
            layer2(U - 1, (U - 1) % 4, E - 1)
            layer3(U - 3, (U - 3) % 4, E - 2)
            layer3(U - 2, (U - 2) % 4, E - 1, stop=True)
            layer3(U - 1, (U - 1) % 4, E - 1, stop=True)
            pe.wait_ge(k_q_ready, 1)
            for h in range(2):
                pe.wait_ge(cond_q_ready, h + 1)
                for c in range(HT):
                    last = pe.matmul(misc[h][:, c * P:(c + 1) * P], cond_q[:, h, c * P:(c + 1) * P], k_q[:, :],
                                     start=True, stop=True)
                last.then_inc(y_ps, 1)


INPUTS = ["x", "cond_256", "L0_cond_rms_w", "L0_cond_wg_W", "L0_cond_wg_b", "L0_cond_gg_W", "L0_cond_gg_b",
          "L0_cond_W1", "L0_cond_b1", "L0_cond_W2", "L0_cond_b2", "L0_cond_W3", "L0_cond_b3",
          "L0_ffn_kernel", "L0_ffn_input_scale", "L0_ffn_kernel_scale", "L0_ffn_bias"]


def kernel(**inputs):
    import numpy as np
    import concourse.bacc as bacc
    from concourse.bass_utils import run_bass_kernel_spmd

    nc = bacc.Bacc("TRN2", target_bir_lowering=False, num_devices=1)
    arrays, args = {}, []
    for name in INPUTS:
        a = np.ascontiguousarray(inputs[name])
        arrays[f"in_{name}_dram"] = a
        args.append(nc.dram_tensor(f"in_{name}_dram", a.shape, mybir.dt.from_np(a.dtype), kind="ExternalInput").ap())
    args.append(nc.dram_tensor("out_0_dram", inputs["x"].shape, F32, kind="ExternalOutput").ap())
    adaln_ffn(nc, *args)
    r = run_bass_kernel_spmd(nc, [arrays], core_ids=[0])
    return r.results[0]["out_0_dram"]
```

```python
from contextlib import ExitStack

import concourse.bass as bass
from concourse import mybir
from concourse.alu_op_type import AluOpType as ALU

ACT = mybir.ActivationFunctionType
AX = mybir.AxisListType
F32 = mybir.dt.float32
F32R = mybir.dt.float32r
BF16 = mybir.dt.bfloat16
I32 = mybir.dt.int32

P = 128
WARM_UP = 6
EPS = 1e-6
EXPONENT_BITS = 0x7F800000
F8_LEAST_NORMAL = 2.0 ** -6
F8_ROUNDER = 1.5 * 2.0 ** 20
F8_LARGEST = 464.0
BF16_OVERFLOW = 7.319348e35


def adaln_ffn(nc, x, cond, rms_w, wg_W, wg_b, gg_W, gg_b, W1, b1, W2, b2, W3, b3,
              ffn_kernel, input_scale, kernel_scale, ffn_bias, out):
    B, S, H = x.shape
    E, _, M = W1.shape
    G = gg_W.shape[0]
    T = B * S // P
    HT = T // 2
    N = HT * P
    MT = M // P
    U = 2 * E
    PB = P // B
    assert (H, B, MT, N, G, E) == (P, 2, 2, 512, 32, 8)
    LOOP_FROM, LOOP_TURNS = 4, 2
    LOOP_END = LOOP_FROM + 4 * LOOP_TURNS

    x_tokens = x.rearrange("b (q t) h -> (b q) t h", t=T)
    out_tokens = out.rearrange("b (q t) h -> (b q) t h", t=T)

    TAIL = {U - 4: (E - 2, 0), U - 3: (E - 1, 0), U - 2: (E - 2, 1), U - 1: (E - 1, 1)}

    def place(u):
        expert, half = TAIL.get(u, (u // 2, u % 2))
        return expert, expert % 2, half, u % 2

    def loop_place(i, n):
        return i * 2 + n // 2, n // 2 % 2, n % 2, n % 2

    def wait(engine, sem, value):
        if not isinstance(value, int) or value > 0:
            engine.wait_ge(sem, value)

    with ExitStack() as ctx:
        def sb(name, shape, dt):
            return ctx.enter_context(nc.sbuf_tensor(name, shape, dt))

        def sem(name):
            return ctx.enter_context(nc.semaphore(name))

        x_tok = sb("x_tok", [P, T, H], F32)
        x_hi = sb("x_hi", [P, 2, N], F32R)
        x_lo = sb("x_lo", [P, 2, N], F32R)
        ident = sb("ident", [P, P], F32)
        w_raw = [sb("w1_raw", [P, 2, 1, M], F32), sb("w2_raw", [P, 2, MT, M], F32), sb("w3_raw", [P, 2, MT, H], F32)]
        w_hi = [sb("w1_hi", [P, 2, 1, M], F32R), sb("w2_hi", [P, 2, MT, M], F32R), sb("w3_hi", [P, 2, MT, H], F32R)]
        w_lo = [sb("w1_lo", [P, 2, 1, M], F32R), sb("w2_lo", [P, 2, MT, M], F32R), sb("w3_lo", [P, 2, MT, H], F32R)]
        bias_rows = sb("bias_rows", [2 * E * MT, P], F32)
        bias_cols = sb("bias_cols", [P, 2, E, MT], F32)
        bias_slot = sb("bias_slot", [P, 2, 2, MT], F32)
        b3_sb = sb("b3_sb", [E, H], F32)
        h1 = sb("h1", [P, 2, MT, N], F32)
        h1_hi = sb("h1_hi", [P, 2, MT, N], F32R)
        h1_lo = sb("h1_lo", [P, 2, MT, N], F32R)
        h2 = sb("h2", [P, 2, MT, N], F32)
        h2_cw = sb("h2_cw", [P, MT, N], F32)
        h2_hi = sb("h2_hi", [P, 2, MT, N], F32R)
        h2_lo = sb("h2_lo", [P, 2, MT, N], F32R)
        warm = sb("warm", [P, N], BF16)
        x_sq = sb("x_sq", [P, T, H], F32)
        sum_sq = sb("sum_sq", [P, T], F32)
        var_eps = sb("var_eps", [P, T], F32)
        minus_half = sb("minus_half", [P, T], F32)
        inv_rms = sb("inv_rms", [P, T], F32)
        rms_col = sb("rms_col", [P, 1], F32)
        wg_raw = sb("wg_raw", [P, E], F32)
        wg_scaled = sb("wg_scaled", [P, E], F32)
        wg_hi = sb("wg_hi", [P, E], F32R)
        wg_lo = sb("wg_lo", [P, E], F32R)
        condT = sb("condT", [G, B], F32)
        genre_lhs = sb("genre_lhs", [G + 2, P], F32)
        genre_rhs = sb("genre_rhs", [G + 2, E], F32)
        gate_bias = sb("gate_bias", [P, E], F32)
        order = sb("order", [P, T, E], F32)
        logits = sb("logits", [P, T, E], F32)
        shifted = sb("shifted", [P, T, E], F32)
        top = sb("top", [P, T], F32)
        prob = sb("prob", [P, T, E], F32)
        prob_sum = sb("prob_sum", [P, T], F32)
        prob_inv = sb("prob_inv", [P, T], F32)
        second = sb("second", [P, T], F32)
        ties = sb("ties", [P, T, E], F32)
        first_of = sb("first_of", [P, T], F32)
        chosen1 = sb("chosen1", [P, T, E], F32)
        chosen2 = sb("chosen2", [P, T, E], F32)
        rest = sb("rest", [P, T, E], F32)
        cw = sb("cw", [P, T, E], F32)
        cw_T = sb("cw_T", [E, T * P], F32)
        cw_row = sb("cw_row", [1, E, T * P], F32)
        cw_bc = sb("cw_bc", [P, E, T * P], F32)
        s_in = sb("s_in", [P, 1], F32)
        s_k = sb("s_k", [P, 1], F32)
        s_hi = sb("s_hi", [P, 2], F32R)
        s_lo = sb("s_lo", [P, 2], F32)
        inv = sb("inv", [P, 2], F32)
        inv_hi = sb("inv_hi", [P, 2], F32R)
        inv_rest = sb("inv_rest", [P, 2], F32)
        inv_err = sb("inv_err", [P, 2], F32)
        inv_lo = sb("inv_lo", [P, 2], F32)
        one = sb("one", [P, 2], F32)
        s_both = sb("s_both", [P, 1], F32)
        k_raw = sb("k_raw", [P, H], BF16)
        k_q = sb("k_q", [P, H], BF16)
        bias_bc = sb("bias_bc", [P, H], BF16)
        first_mix = sb("first_mix", [P, 2, N], F32)
        cond_out = sb("cond_out", [P, 2, N], BF16)
        zeros = sb("zeros", [P, H], BF16)
        q_a = sb("q_a", [P, 2, N], F32)
        q_v = sb("q_v", [P, 2, N], F32)
        q_m = sb("q_m", [P, 2, N], I32)
        q_r = sb("q_r", [P, 2, N], F32)
        q_s = sb("q_s", [P, 2, N], F32)
        cond_q = sb("cond_q", [P, 2, N], BF16)
        nan_q = sb("nan_q", [P, 2, N], BF16)
        k_nan = sb("k_nan", [P, H], BF16)
        y_bf = sb("y_bf", [P, 2, N], BF16)
        y_biased = sb("y_biased", [P, 2, N], BF16)
        y_out = sb("y_out", [P, 2, N], F32)

        def bank(name):
            return ctx.enter_context(nc.psum_tensor(name, [P, N], F32))

        acc = [bank("acc0"), bank("acc1")]
        z1 = [bank("z1_0"), bank("z1_1")]
        z2 = [bank("z2_0"), bank("z2_1")]
        misc = [bank("misc0"), bank("misc1")]

        x_loaded = [sem("x_loaded0"), sem("x_loaded1")]
        w_loaded = [[sem(f"w{l + 1}_loaded{p}") for p in range(2)] for l in range(3)]
        gate_w_loaded = sem("gate_w_loaded")
        genre_loaded = sem("genre_loaded")
        bias_loaded = sem("bias_loaded")
        b3_loaded = sem("b3_loaded")
        ffn_loaded = sem("ffn_loaded")
        ffn_bias_loaded = sem("ffn_bias_loaded")
        warm_ready = sem("warm_ready")
        zeroed = sem("zeroed")
        ident_ready = sem("ident_ready")
        consts_ready = sem("consts_ready")
        genre_lhs_ready = sem("genre_lhs_ready")
        xT_ready = sem("xT_ready")
        x_hi_ready = sem("x_hi_ready")
        x_lo_ready = sem("x_lo_ready")
        x_sq_ready = sem("x_sq_ready")
        var_ready = sem("var_ready")
        inv_rms_ready = sem("inv_rms_ready")
        wg_split = sem("wg_split")
        gate_bias_ps = sem("gate_bias_ps")
        gate_bias_ready = sem("gate_bias_ready")
        bias_cols_ps = sem("bias_cols_ps")
        logits_ps = sem("logits_ps")
        shifted_ready = sem("shifted_ready")
        prob_ready = sem("prob_ready")
        cw_ready = sem("cw_ready")
        cwT_ps = sem("cwT_ps")
        cwT_ready = sem("cwT_ready")
        cw_row_loaded = sem("cw_row_loaded")
        cw_bc_ready = sem("cw_bc_ready")
        w_hi_ready = [sem(f"w{l + 1}_hi_ready") for l in range(3)]
        w_lo_ready = [sem(f"w{l + 1}_lo_ready") for l in range(3)]
        bias_slot_ready = sem("bias_slot_ready")
        z1_ready = sem("z1_ready")
        z2_ready = sem("z2_ready")
        l3_done = sem("l3_done")
        h1_ready = sem("h1_ready")
        h1_hi_ready = sem("h1_hi_ready")
        h1_lo_ready = sem("h1_lo_ready")
        h2_ready = sem("h2_ready")
        h2_scaled = sem("h2_scaled")
        h2_hi_ready = sem("h2_hi_ready")
        h2_lo_ready = sem("h2_lo_ready")
        last_lo_ready = sem("last_lo_ready")
        dve_chain = sem("dve_chain")
        k_q_ready = sem("k_q_ready")
        first_mixed = sem("first_mixed")
        scales_ready = sem("scales_ready")
        cond_ready, qa_ready, qv_ready, qm_ready, qr_ready, qs_ready, cond_q_ready = (
            sem(n) for n in ("cond_ready", "qa_ready", "qv_ready", "qm_ready", "qr_ready", "qs_ready", "cond_q_ready"))
        piece_chain = [sem("piece_chain0"), sem("piece_chain1")]
        QUOTIENT, ROUNDED = 3, 7
        nan_ready = [sem("nan_ready0"), sem("nan_ready1")]
        y_ps = [sem("y_ps0"), sem("y_ps1")]
        y_bf_ready = [sem("y_bf_ready0"), sem("y_bf_ready1")]
        y_out_ready = [sem("y_out_ready0"), sem("y_out_ready1")]
        stored = sem("stored")

        PIECES = ((0, 0, N), (1, 0, N // 2), (1, N // 2, N))
        OUT_ORDER = ((0, 0, N, 1), (1, 0, N // 2, 1), (1, N // 2, N, 2))
        y_bank = {(0, 0): misc[0], (1, 0): misc[1], (1, N // 2): z1[0]}

        block = ctx.enter_context(nc.Block())

        @block.sync
        def _(sp):
            def load_weights(l, expert, slot):
                W = (W1, W2, W3)[l]
                src = W[expert:expert + 1, :, :] if isinstance(expert, int) else W[bass.ds(expert, 1), :, :]
                sp.dma_start(w_raw[l][:, slot, :, :], src.rearrange("e (k p) n -> p (e k) n", p=P))\
                    .then_inc(w_loaded[l][slot], 16)

            sp.dma_start(x_tok[:, 0:HT, :], x_tokens[:, 0:HT, :]).then_inc(x_loaded[0], 16)
            load_weights(0, 0, 0)
            sp.dma_start(x_tok[:, HT:T, :], x_tokens[:, HT:T, :]).then_inc(x_loaded[1], 16)
            sp.dma_start(bias_rows[0:E * MT, :], b1.rearrange("e (m p) -> (e m) p", p=P)).then_inc(bias_loaded, 16)
            sp.dma_start(bias_rows[E * MT:2 * E * MT, :], b2.rearrange("e (m p) -> (e m) p", p=P)).then_inc(bias_loaded, 16)
            load_weights(1, 0, 0)
            load_weights(0, 1, 1)
            load_weights(2, 0, 0)
            load_weights(1, 1, 1)
            load_weights(2, 1, 1)
            with sp.Fori(0, (E - 2) // 2) as i:
                for slot in range(2):
                    for l in (0, 1, 2):
                        sp.wait_ge(w_lo_ready[l], i * 2 + (slot + 1))
                        load_weights(l, i * 2 + (2 + slot), slot)
            for h, c0, c1, n in OUT_ORDER:
                t0, t1 = h * HT + c0 // P, h * HT + c1 // P
                sp.wait_ge(y_out_ready[h], n)
                sp.dma_start(out_tokens[:, t0:t1, :], y_out[:, h, c0:c1].rearrange("p (t f) -> p t f", f=H))\
                    .then_inc(stored, 16)
            sp.wait_ge(stored, 16 * len(PIECES))

        @block.gpsimd
        def _(pool):
            pool.memset(ident[:, :], 0.0).then_inc(zeroed, 1)
            pool.wait_ge(zeroed, 1)
            pool.affine_select(out=ident[:, :], in_=ident[:, :], compare_op=ALU.not_equal, fill=1.0, base=0,
                               pattern=[[-1, P]], channel_multiplier=1).then_inc(ident_ready, 1)
            pool.memset(genre_lhs[:, :], 1.0).then_inc(consts_ready, 1)
            pool.memset(minus_half[:, :], -0.5).then_inc(consts_ready, 1)
            for e in range(E):
                pool.memset(order[:, :, e:e + 1], float(E - e)).then_inc(consts_ready, 1)
            pool.dma_start(condT[:, :], cond.rearrange("b g -> g b"), allow_slow_non_contiguous=True).then_inc(genre_loaded, 16)
            pool.dma_start(genre_rhs[0:G, :], gg_W).then_inc(genre_loaded, 16)
            pool.dma_start(genre_rhs[G:G + 1, :], wg_b.rearrange("(o e) -> o e", o=1)).then_inc(genre_loaded, 16)
            pool.dma_start(genre_rhs[G + 1:G + 2, :], gg_b.rearrange("(o e) -> o e", o=1)).then_inc(genre_loaded, 16)

            def low_part(l, expert, slot):
                pool.wait_ge(w_hi_ready[l], expert + 1)
                pool.tensor_tensor(w_lo[l][:, slot, :, :], w_raw[l][:, slot, :, :],
                                   w_hi[l][:, slot, :, :].bitcast(F32), ALU.subtract).then_inc(w_lo_ready[l], 1)

            low_part(0, 0, 0)
            pool.wait_ge(x_loaded[1], 16)
            part = x_tok[:, HT:T, :]
            pool.tensor_tensor(x_sq[:, HT:T, :], part, part, ALU.mult).then_inc(x_sq_ready, 1)
            low_part(1, 0, 0)
            pool.wait_ge(consts_ready, 2)
            pool.wait_ge(var_ready, 1)
            pool.tensor_tensor(inv_rms[:, :], var_eps[:, :], minus_half[:, :], ALU.pow).then_inc(inv_rms_ready, 1)
            low_part(0, 1, 1)
            pool.dma_start(b3_sb[:, :], b3).then_inc(b3_loaded, 16)
            pool.dma_start(k_raw[:, :], ffn_kernel).then_inc(ffn_loaded, 16)
            pool.dma_start(s_in[:, :], input_scale.partition_broadcast(P)).then_inc(ffn_loaded, 16)
            pool.dma_start(s_k[:, :], kernel_scale.partition_broadcast(P)).then_inc(ffn_loaded, 16)
            pool.dma_start(bias_bc[:, :], ffn_bias.partition_broadcast(P)).then_inc(ffn_bias_loaded, 16)

            low_part(1, 1, 1)
            low_part(0, 2, 0)
            low_part(2, 0, 0)
            pool.wait_ge(cwT_ready, 2)
            pool.dma_start(cw_row[0:1, :, :], cw_T[:, :]).then_inc(cw_row_loaded, 16)
            low_part(1, 2, 0)
            pool.wait_ge(cw_row_loaded, 16)
            pool.partition_broadcast(cw_bc[:, 1, :], cw_row[0:1, 1, :], P).then_inc(cw_bc_ready, 1)
            pool.partition_broadcast(cw_bc[:, 0, :], cw_row[0:1, 0, :], P).then_inc(cw_bc_ready, 1)
            pool.partition_broadcast(cw_bc[:, 2, :], cw_row[0:1, 2, :], P).then_inc(cw_bc_ready, 1)
            low_part(0, 3, 1)
            low_part(2, 1, 1)
            pool.partition_broadcast(cw_bc[:, 3, :], cw_row[0:1, 3, :], P).then_inc(cw_bc_ready, 1)
            low_part(1, 3, 1)
            for e in range(4, E):
                pool.partition_broadcast(cw_bc[:, e, :], cw_row[0:1, e, :], P).then_inc(cw_bc_ready, 1)
            with pool.Fori(0, LOOP_TURNS) as i:
                for s in range(LOOP_FROM, LOOP_FROM + 4):
                    k, slot = i * 2 + s // 2, s // 2 % 2
                    if s % 2 == 0:
                        low_part(0, k + 2, slot)
                        low_part(2, k, slot)
                    else:
                        low_part(1, k + 2, slot)
            low_part(2, E - 2, 0)
            low_part(2, E - 1, 1)
            pool.wait_ge(qr_ready, 1)
            pool.tensor_tensor(q_s[:, 0, :], q_v[:, 0, :], q_r[:, 0, :], ALU.add).then_inc(qs_ready, 1)
            pool.wait_ge(qs_ready, 1)
            pool.tensor_tensor(cond_q[:, 0, :], q_s[:, 0, :], q_r[:, 0, :], ALU.subtract).then_inc(cond_q_ready, 1)

        @block.scalar
        def _(act):
            act.dma_start(wg_raw[:, :], wg_W).then_inc(gate_w_loaded, 16)
            act.dma_start(rms_col[:, :], rms_w.rearrange("(p o) -> p o", o=1)).then_inc(gate_w_loaded, 16)

            def high_part(l, expert, nth, slot):
                act.wait_ge(w_loaded[l][slot], nth * 16)
                if not isinstance(expert, int) or expert >= 2:
                    used, per_expert = ((z1_ready, 2 * MT), (z2_ready, 2 * MT), (l3_done, 2))[l]
                    act.wait_ge(used, (expert - 1) * per_expert)
                act.activation(w_hi[l][:, slot, :, :], w_raw[l][:, slot, :, :], ACT.Copy).then_inc(w_hi_ready[l], 1)

            def relu1(u, bias_count, at):
                _, w_slot, _, slot = at
                act.wait_ge(bias_slot_ready, bias_count)
                wait(act, h1_lo_ready, u - 1)
                for m in range(MT):
                    act.wait_ge(z1_ready, u * 2 + (m + 1))
                    act.activation(h1[:, slot, m, :], z1[m][:, :], ACT.Relu, bias=bias_slot[:, w_slot, 0, m:m + 1])\
                        .then_inc(h1_ready, 1)
                act.wait_ge(h1_ready, u * 2 + 2)
                wait(act, z2_ready, u * 2 - 2)
                act.activation(h1_hi[:, slot, :, :], h1[:, slot, :, :], ACT.Copy).then_inc(h1_hi_ready, 1)

            def relu2(u, at):
                _, w_slot, _, slot = at
                if isinstance(u, int) and u < 4:
                    wait(act, h2_lo_ready, u - 1)
                else:
                    act.wait_ge(h2_scaled, u - 3)
                for m in range(MT):
                    act.wait_ge(z2_ready, u * 2 + (m + 1))
                    act.activation(h2[:, slot, m, :], z2[m][:, :], ACT.Relu, bias=bias_slot[:, w_slot, 1, m:m + 1])\
                        .then_inc(h2_ready, 1)

            high_part(0, 0, 1, 0)
            for h in range(2):
                act.wait_ge(xT_ready, h + 1)
                act.activation(x_hi[:, h, :], misc[h][:, :], ACT.Copy).then_inc(x_hi_ready, 1)
            high_part(1, 0, 1, 0)
            relu1(0, 1, place(0))
            high_part(0, 1, 1, 1)
            act.wait_ge(shifted_ready, 1)
            act.activation(prob[:, :, :], shifted[:, :, :], ACT.Exp).then_inc(prob_ready, 1)
            relu1(1, 1, place(1))
            high_part(1, 1, 1, 1)
            relu2(0, place(0))
            high_part(0, 2, 2, 0)
            high_part(2, 0, 1, 0)
            act.wait_ge(cwT_ps, 2)
            act.activation(cw_T[:, N:2 * N], acc[1][0:E, :], ACT.Copy).then_inc(cwT_ready, 1)
            for s in range(1, LOOP_FROM):
                relu1(s + 1, (s + 1) // 2 + 1, place(s + 1))
                relu2(s, place(s))
                if s % 2 == 0:
                    high_part(0, s // 2 + 2, 2, s // 2 % 2)
                    high_part(2, s // 2, 1, s // 2 % 2)
                else:
                    high_part(1, s // 2 + 2, 2, s // 2 % 2)
            with act.Fori(0, LOOP_TURNS) as i:
                for s in range(LOOP_FROM, LOOP_FROM + 4):
                    relu1(i * 4 + (s + 1), i * 2 + ((s + 1) // 2 + 1), loop_place(i, s + 1))
                    relu2(i * 4 + s, loop_place(i, s))
                    k, slot = i * 2 + s // 2, s // 2 % 2
                    if s % 2 == 0:
                        high_part(0, k + 2, i + ((s // 2 + 2) // 2 + 1), slot)
                        high_part(2, k, i + (s // 2 // 2 + 1), slot)
                    else:
                        high_part(1, k + 2, i + ((s // 2 + 2) // 2 + 1), slot)
            for s in range(LOOP_END, U):
                if s + 1 < U:
                    relu1(s + 1, E, place(s + 1))
                relu2(s, place(s))
                if s in (U - 4, U - 2):
                    expert = E - 2 + (s - (U - 4)) // 2
                    high_part(2, expert, expert // 2 + 1, expert % 2)

            def nan_marks(h, c0, c1, n):
                act.wait_ge(qv_ready if h == 0 else piece_chain[n - 1], 1 if h == 0 else QUOTIENT)
                act.activation(nan_q[:, h, c0:c1], q_v[:, h, c0:c1], ACT.Copy, scale=BF16_OVERFLOW).then_inc(nan_ready[h], 1)

            act.wait_ge(cond_ready, 1)
            act.activation(q_a[:, 0, :], cond_out[:, 0, :], ACT.Copy, scale=inv_lo[:, 0:1]).then_inc(qa_ready, 1)
            for h, c0, c1, n in OUT_ORDER:
                nan_marks(h, c0, c1, n)
            for h, c0, c1, n in OUT_ORDER:
                act.wait_ge(y_ps[h], n)
                act.activation(y_bf[:, h, c0:c1], y_bank[h, c0][:, 0:c1 - c0], ACT.Copy, scale=s_both[:, 0:1])\
                    .then_inc(y_bf_ready[h], 1)

        @block.vector
        def _(dve):
            count = [0]

            def link(instruction):
                count[0] += 1
                instruction.then_inc(dve_chain, 1)
                dve.wait_ge(dve_chain, count[0])

            def per_token(v):
                return v[:, :].unsqueeze(2).to_broadcast([P, T, E])

            def x_low(h):
                dve.wait_ge(x_hi_ready, h + 1)
                dve.tensor_tensor(x_lo[:, h, :], misc[h][:, :], x_hi[:, h, :].bitcast(F32), ALU.subtract)\
                    .then_inc(x_lo_ready, 1)

            dve.memset(warm[:, :], 0.0).then_inc(warm_ready, 1)
            dve.memset(zeros[:, :], 0.0).then_inc(warm_ready, 1)
            dve.memset(one[:, :], 1.0).then_inc(warm_ready, 1)
            dve.wait_ge(x_loaded[0], 16)
            link(dve.tensor_tensor(x_sq[:, 0:HT, :], x_tok[:, 0:HT, :], x_tok[:, 0:HT, :], ALU.mult))
            x_low(0)
            dve.reduce_sum(sum_sq[:, 0:HT], x_sq[:, 0:HT, :], AX.X).then_inc(x_sq_ready, 1)
            dve.wait_ge(gate_w_loaded, 32)
            link(dve.tensor_scalar(wg_scaled[:, :], wg_raw[:, :], rms_col[:, 0:1], None, ALU.mult))
            link(dve.tensor_copy(wg_hi[:, :], wg_scaled[:, :]))
            dve.tensor_tensor(wg_lo[:, :], wg_scaled[:, :], wg_hi[:, :].bitcast(F32), ALU.subtract).then_inc(wg_split, 1)
            x_low(1)
            dve.wait_ge(bias_cols_ps, 1)
            link(dve.tensor_copy(bias_cols[:, :, :, :].rearrange("p l e m -> p (l e m)"), z2[0][:, 0:2 * E * MT]))

            def load_bias_slot(expert, slot):
                src = bias_cols[:, :, expert:expert + 1, :] if isinstance(expert, int) else bias_cols[:, :, bass.ds(expert, 1), :]
                dve.tensor_scalar(bias_slot[:, slot, :, :], src.rearrange("p l o m -> p l (o m)"), 1.0, None, ALU.mult)\
                    .then_inc(bias_slot_ready, 1)

            load_bias_slot(0, 0)
            dve.wait_ge(x_sq_ready, 2)
            link(dve.reduce_sum(sum_sq[:, HT:T], x_sq[:, HT:T, :], AX.X))
            dve.tensor_scalar(var_eps[:, :], sum_sq[:, :], 1.0 / H, EPS, ALU.mult, ALU.add).then_inc(var_ready, 1)
            dve.wait_ge(consts_ready, 2)
            dve.wait_ge(genre_loaded, 64)
            for b in range(B):
                dve.tensor_copy(genre_lhs[0:G, b * PB:(b + 1) * PB], condT[:, b:b + 1].to_broadcast([G, PB]))\
                    .then_inc(genre_lhs_ready, 1)
            load_bias_slot(1, 1)

            def h1_low(u, at):
                slot = at[3]
                dve.wait_ge(h1_hi_ready, u + 1)
                dve.tensor_tensor(h1_lo[:, slot, :, :], h1[:, slot, :, :], h1_hi[:, slot, :, :].bitcast(F32),
                                  ALU.subtract).then_inc(h1_lo_ready, 1)

            dve.wait_ge(gate_bias_ps, 1)
            dve.tensor_copy(gate_bias[:, :], z2[1][:, 0:E]).then_inc(gate_bias_ready, 1)
            dve.wait_ge(inv_rms_ready, 1)
            dve.wait_ge(logits_ps, 1)
            link(dve.tensor_tensor(logits[:, :, :], acc[0][:, 0:T * E].rearrange("p (t e) -> p t e", e=E),
                                   per_token(inv_rms), ALU.mult))
            dve.wait_ge(gate_bias_ready, 1)
            link(dve.tensor_tensor(logits[:, :, :], logits[:, :, :],
                                   gate_bias[:, :].unsqueeze(1).to_broadcast([P, T, E]), ALU.add))
            link(dve.reduce_max(top[:, :], logits[:, :, :], AX.X))
            dve.tensor_tensor(shifted[:, :, :], logits[:, :, :], per_token(top), ALU.subtract).then_inc(shifted_ready, 1)
            dve.wait_ge(consts_ready, 2 + E)

            def choose(of, largest, chosen):
                link(dve.tensor_tensor(ties[:, :, :], of[:, :, :], per_token(largest), ALU.is_equal))
                link(dve.tensor_tensor(ties[:, :, :], ties[:, :, :], order[:, :, :], ALU.mult))
                link(dve.reduce_max(first_of[:, :], ties[:, :, :], AX.X))
                link(dve.tensor_tensor(chosen[:, :, :], ties[:, :, :], per_token(first_of), ALU.is_equal))

            choose(logits, top, chosen1)
            h1_low(0, place(0))
            link(dve.scalar_tensor_tensor(rest[:, :, :], chosen1[:, :, :], -3.0e38, logits[:, :, :], ALU.mult, ALU.add))
            link(dve.reduce_max(second[:, :], rest[:, :, :], AX.X))
            choose(rest, second, chosen2)
            link(dve.tensor_tensor(chosen1[:, :, :], chosen1[:, :, :], chosen2[:, :, :], ALU.add))
            dve.wait_ge(prob_ready, 1)
            link(dve.reduce_sum(prob_sum[:, :], prob[:, :, :], AX.X))
            dve.tensor_tensor(cw[:, :, :], prob[:, :, :], chosen1[:, :, :], ALU.mult)
            link(dve.reciprocal(prob_inv[:, :], prob_sum[:, :]))
            dve.tensor_tensor(cw[:, :, :], cw[:, :, :], per_token(prob_inv), ALU.mult).then_inc(cw_ready, 1)
            h1_low(1, place(1))
            dve.wait_ge(cwT_ps, 1)
            dve.tensor_copy(cw_T[:, 0:N], acc[0][0:E, :]).then_inc(cwT_ready, 1)

            def split_h2(u, at):
                expert, _, half, slot = at
                src = h2[:, slot, :, :]
                dve.wait_ge(h2_ready, u * 2 + 2)
                if not isinstance(expert, int) or expert > 0:
                    dve.wait_ge(cw_bc_ready, 1 if isinstance(expert, int) and expert == 1 else expert + 1)
                    which = slice(expert, expert + 1) if isinstance(expert, int) else bass.ds(expert, 1)
                    mix = cw_bc[:, which, half * N:(half + 1) * N].to_broadcast([P, MT, N])
                    dve.wait_ge(h2_lo_ready, u)
                    dve.tensor_tensor(h2_cw[:, :, :], h2[:, slot, :, :], mix, ALU.mult).then_inc(h2_scaled, 1)
                    dve.wait_ge(h2_scaled, u - 1)
                    dve.wait_ge(l3_done, u - 1)
                    src = h2_cw[:, :, :]
                dve.tensor_copy(h2_hi[:, slot, :, :], src).then_inc(h2_hi_ready, 1)
                dve.wait_ge(h2_hi_ready, u + 1)
                dve.tensor_tensor(h2_lo[:, slot, :, :], src, h2_hi[:, slot, :, :].bitcast(F32),
                                  ALU.subtract).then_inc(h2_lo_ready, 1)

            def mix_first(h):
                dve.wait_ge(l3_done, h + 1)
                dve.wait_ge(cw_bc_ready, 2)
                dve.tensor_tensor(first_mix[:, h, :], misc[h][:, :], cw_bc[:, 0, h * N:(h + 1) * N], ALU.mult)\
                    .then_inc(first_mixed, 1)

            h1_low(2, place(2))
            split_h2(0, place(0))
            dve.wait_ge(ffn_loaded, 48)
            dve.wait_ge(warm_ready, 3)
            for c, s in enumerate((s_in, s_k)):
                col = slice(c, c + 1)
                dve.tensor_copy(s_hi[:, col], s[:, :])
                link(dve.reciprocal(inv[:, col], s[:, :]))
                dve.tensor_tensor(s_lo[:, col], s[:, :], s_hi[:, col].bitcast(F32), ALU.subtract)
                link(dve.tensor_copy(inv_hi[:, col], inv[:, col]))
                link(dve.tensor_tensor(inv_rest[:, col], inv[:, col], inv_hi[:, col].bitcast(F32), ALU.subtract))
                for n, (a, b) in enumerate(((s_hi, inv_hi), (s_hi, inv_rest), (s_lo, inv_hi), (s_lo, inv_rest))):
                    a_part = a[:, col].bitcast(F32) if a is s_hi else a[:, col]
                    b_part = b[:, col].bitcast(F32) if b is inv_hi else b[:, col]
                    before = one if n == 0 else inv_err
                    link(dve.scalar_tensor_tensor(inv_err[:, col], a_part, b_part, before[:, col], ALU.mult,
                                                  ALU.subtract if n == 0 else ALU.add))
                link(dve.tensor_tensor(inv_err[:, col], inv_err[:, col], inv[:, col], ALU.mult))
                link(dve.tensor_tensor(inv_lo[:, col], inv_rest[:, col], inv_err[:, col], ALU.subtract))
            dve.tensor_tensor(s_both[:, :], s_in[:, :], s_k[:, :], ALU.mult).then_inc(scales_ready, 1)

            def low_quotient(a, v_lo, c):
                return dve.tensor_scalar(v_lo, a, inv_lo[:, c:c + 1], None, ALU.mult)

            def quotient(a, v_lo, v, c):
                return dve.scalar_tensor_tensor(v, a, inv_hi[:, c:c + 1].bitcast(F32), v_lo, ALU.mult, ALU.add)

            def exponent(v, m):
                return dve.tensor_scalar(m, v.bitcast(I32), EXPONENT_BITS, None, ALU.bitwise_and)

            def rounder(m, r):
                return dve.tensor_scalar(r, m.bitcast(F32), F8_LEAST_NORMAL, F8_ROUNDER, ALU.max, ALU.mult)

            k_a, k_v, k_m, k_r, k_s = (a[:, 0, 0:H] for a in (q_a, q_v, q_m, q_r, q_s))
            link(low_quotient(k_raw[:, :], k_a, 1))
            link(quotient(k_raw[:, :], k_a, k_v, 1))
            dve.tensor_scalar(k_nan[:, :], k_v, BF16_OVERFLOW, None, ALU.mult)
            link(exponent(k_v, k_m))
            link(rounder(k_m, k_r))
            link(dve.tensor_tensor(k_s, k_v, k_r, ALU.add))
            dve.tensor_tensor(k_s, k_s, k_r, ALU.subtract)
            link(dve.tensor_scalar(k_nan[:, :], k_nan[:, :], 0.0, None, ALU.mult))
            dve.tensor_tensor(k_q[:, :], k_s, k_nan[:, :], ALU.add).then_inc(k_q_ready, 1)

            def biases_due(k, slot):
                dve.wait_ge(h2_ready, k * 4)
                load_bias_slot(k + 1, slot)

            biases_due(1, 0)
            h1_low(3, place(3))
            split_h2(1, place(1))
            h1_low(4, place(4))
            split_h2(2, place(2))
            mix_first(0)
            with dve.Fori(0, LOOP_TURNS) as i:
                for s in range(LOOP_FROM, LOOP_FROM + 4):
                    if s % 2 == 0:
                        biases_due(i * 2 + s // 2, (s // 2 + 1) % 2)
                    h1_low(i * 4 + (s + 1), loop_place(i, s + 1))
                    split_h2(i * 4 + (s - 1), loop_place(i, s - 1))
            biases_due(E - 2, 1)
            for s in range(LOOP_END, U):
                if s + 1 < U:
                    h1_low(s + 1, place(s + 1))
                split_h2(s - 1, place(s - 1))
                if s == LOOP_END:
                    mix_first(1)
            u = U - 1
            expert, _, half, slot = place(u)
            dve.wait_ge(l3_done, u - 1)
            dve.wait_ge(h2_lo_ready, u)
            for m in range(MT):
                dve.wait_ge(h2_ready, u * 2 + m + 1)
                dve.tensor_tensor(h2_cw[:, m, :], h2[:, slot, m, :], cw_bc[:, expert, half * N:(half + 1) * N],
                                  ALU.mult).then_inc(h2_scaled, 1)
                dve.wait_ge(h2_scaled, u - 1 + m)
                dve.tensor_copy(h2_hi[:, slot, m, :], h2_cw[:, m, :]).then_inc(h2_hi_ready, 1)
                dve.wait_ge(h2_hi_ready, u + 1 + m)
                dve.tensor_tensor(h2_lo[:, slot, m, :], h2_cw[:, m, :], h2_hi[:, slot, m, :].bitcast(F32),
                                  ALU.subtract).then_inc(last_lo_ready, 1)

            def mixture(h, c0, c1):
                return dve.tensor_tensor(cond_out[:, h, c0:c1], acc[h][:, c0:c1], first_mix[:, h, c0:c1], ALU.add)

            ends = PIECES[1:]
            done = [0] * len(ends)

            def by_turns(stage, extra=None):
                for n, (_, c0, c1) in enumerate(ends):
                    if done[n]:
                        dve.wait_ge(piece_chain[n], done[n])
                    stage(slice(c0, c1)).then_inc(piece_chain[n], 1)
                    done[n] += 1

            dve.wait_ge(l3_done, U - 2)
            dve.wait_ge(first_mixed, 2)
            mixture(0, 0, N).then_inc(cond_ready, 1)
            dve.wait_ge(l3_done, U)
            by_turns(lambda c: mixture(1, c.start, c.stop))
            dve.wait_ge(scales_ready, 1)
            dve.wait_ge(cond_ready, 1)
            dve.wait_ge(qa_ready, 1)
            quotient(cond_out[:, 0, :], q_a[:, 0, :], q_v[:, 0, :], 0).then_inc(qv_ready, 1)
            by_turns(lambda c: low_quotient(cond_out[:, 1, c], q_a[:, 1, c], 0))
            dve.wait_ge(qv_ready, 1)
            exponent(q_v[:, 0, :], q_m[:, 0, :]).then_inc(qm_ready, 1)
            by_turns(lambda c: quotient(cond_out[:, 1, c], q_a[:, 1, c], q_v[:, 1, c], 0))
            dve.wait_ge(qm_ready, 1)
            rounder(q_m[:, 0, :], q_r[:, 0, :]).then_inc(qr_ready, 1)
            by_turns(lambda c: exponent(q_v[:, 1, c], q_m[:, 1, c]))
            by_turns(lambda c: rounder(q_m[:, 1, c], q_r[:, 1, c]))
            by_turns(lambda c: dve.tensor_tensor(q_s[:, 1, c], q_v[:, 1, c], q_r[:, 1, c], ALU.add))
            by_turns(lambda c: dve.tensor_tensor(cond_q[:, 1, c], q_s[:, 1, c], q_r[:, 1, c], ALU.subtract))
            dve.wait_ge(ffn_bias_loaded, 16)
            for h, c0, c1, n in OUT_ORDER:
                nt = (c1 - c0) // P
                t0 = h * HT + c0 // P
                dve.wait_ge(y_bf_ready[h], n)
                link(dve.tensor_tensor(y_biased[:, h, c0:c1].rearrange("p (t f) -> p t f", f=H),
                                       y_bf[:, h, c0:c1].rearrange("p (t f) -> p t f", f=H),
                                       bias_bc[:, :].unsqueeze(1).to_broadcast([P, nt, H]), ALU.add))
                dve.tensor_tensor(y_out[:, h, c0:c1], y_biased[:, h, c0:c1],
                                  x_tok[:, t0:t0 + nt, :].rearrange("p t f -> p (t f)"), ALU.add)\
                    .then_inc(y_out_ready[h], 1)

        @block.tensor
        def _(pe):
            pe.wait_ge(warm_ready, 1)
            for _ in range(WARM_UP):
                pe.matmul(z1[1][:, :], warm[:, 0:P], warm[:, :], start=True, stop=True)
            pe.wait_ge(ident_ready, 1)

            def transpose_x(h):
                pe.wait_ge(x_loaded[h], 16)
                for c in range(HT):
                    last = pe.transpose(misc[h][:, c * P:(c + 1) * P], x_tok[:, h * HT + c, :], ident[:, :])
                last.then_inc(xT_ready, 1)

            def products(bank, parts, start, stop):
                n, passes = 0, 3 * len(parts)
                for wh, wl, mh, ml in parts:
                    for a, b in ((wh, mh), (wh, ml), (wl, mh)):
                        last = pe.matmul(bank, a, b, start=start and n == 0, stop=stop and n == passes - 1)
                        n += 1
                return last

            def layer1(u, at, new_expert):
                expert, w_slot, half, _ = at
                if new_expert:
                    pe.wait_ge(w_lo_ready[0], expert + 1)
                for m in range(MT):
                    wait(pe, h1_ready, u * 2 + (m - 1))
                    cols = slice(m * P, (m + 1) * P)
                    products(z1[m][:, :], [(w_hi[0][:, w_slot, 0, cols], w_lo[0][:, w_slot, 0, cols],
                                            x_hi[:, half, :], x_lo[:, half, :])], True, True).then_inc(z1_ready, 1)

            def layer2(u, at, new_expert):
                expert, w_slot, _, slot = at
                if new_expert:
                    pe.wait_ge(w_lo_ready[1], expert + 1)
                pe.wait_ge(h1_lo_ready, u + 1)
                for m in range(MT):
                    wait(pe, h2_ready, u * 2 + (m - 1))
                    cols = slice(m * P, (m + 1) * P)
                    products(z2[m][:, :], [(w_hi[1][:, w_slot, k, cols], w_lo[1][:, w_slot, k, cols],
                                            h1_hi[:, slot, k, :], h1_lo[:, slot, k, :]) for k in range(MT)],
                             True, True).then_inc(z2_ready, 1)

            def layer3(u, at, new_expert, stop=False):
                expert, w_slot, half, slot = at
                first = isinstance(expert, int) and expert == 0
                if new_expert:
                    pe.wait_ge(w_lo_ready[2], expert + 1)
                pe.wait_ge(h2_lo_ready, u + 1)
                products((misc if first else acc)[half][:, :],
                         [(w_hi[2][:, w_slot, k, :], w_lo[2][:, w_slot, k, :],
                           h2_hi[:, slot, k, :], h2_lo[:, slot, k, :]) for k in range(MT)],
                         first, first or stop).then_inc(l3_done, 1)

            transpose_x(0)
            transpose_x(1)
            pe.wait_ge(bias_loaded, 32)
            nb = 2 * E * MT
            pe.transpose(z2[0][:, 0:nb], bias_rows[:, :], ident[0:nb, 0:nb]).then_inc(bias_cols_ps, 1)
            pe.wait_ge(x_lo_ready, 1)
            layer1(0, place(0), True)
            pe.wait_ge(wg_split, 1)
            pe.wait_ge(x_lo_ready, 2)
            for c in range(T):
                hi = x_hi[:, c // HT, (c % HT) * P:(c % HT + 1) * P]
                lo = x_lo[:, c // HT, (c % HT) * P:(c % HT + 1) * P]
                for n, (a, b) in enumerate(((hi, wg_hi), (hi, wg_lo), (lo, wg_hi))):
                    last = pe.matmul(acc[0][:, c * E:(c + 1) * E], a, b[:, :], start=n == 0, stop=n == 2)
            last.then_inc(logits_ps, 1)
            pe.wait_ge(genre_lhs_ready, 2)
            pe.matmul(z2[1][:, 0:E], genre_lhs[:, :], genre_rhs[:, :], start=True, stop=True).then_inc(gate_bias_ps, 1)
            layer1(1, place(1), False)
            pe.wait_ge(bias_slot_ready, 1)
            pe.wait_ge(gate_bias_ready, 1)
            layer2(0, place(0), True)
            layer1(2, place(2), True)
            layer2(1, place(1), False)
            pe.wait_ge(cw_ready, 1)
            for h in range(2):
                for c in range(HT):
                    last = pe.transpose(acc[h][0:E, c * P:(c + 1) * P], cw[:, h * HT + c, :], ident[:, :])
                last.then_inc(cwT_ps, 1)
            for s in range(2, LOOP_FROM):
                layer1(s + 1, place(s + 1), s % 2 == 1)
                layer2(s, place(s), s % 2 == 0)
                layer3(s - 2, place(s - 2), s % 2 == 0)
            pe.wait_ge(b3_loaded, 16)
            pe.wait_ge(cwT_ready, 2)
            for h in range(2):
                pe.matmul(acc[h][:, :], b3_sb[:, :], cw_T[:, h * N:(h + 1) * N], start=True, stop=False)
            with pe.Fori(0, LOOP_TURNS) as i:
                for s in range(LOOP_FROM, LOOP_FROM + 4):
                    layer1(i * 4 + (s + 1), loop_place(i, s + 1), s % 2 == 1)
                    layer2(i * 4 + s, loop_place(i, s), s % 2 == 0)
                    layer3(i * 4 + (s - 2), loop_place(i, s - 2), s % 2 == 0)
            for s in range(LOOP_END, U):
                if s + 1 < U:
                    layer1(s + 1, place(s + 1), s == LOOP_END)
                layer2(s, place(s), s in (LOOP_END, LOOP_END + 1))
                layer3(s - 2, place(s - 2), s in (LOOP_END, LOOP_END + 2, LOOP_END + 3), stop=place(s - 2)[0] == E - 1)
            layer3(U - 2, place(U - 2), False)
            _, w_slot, half, slot = place(U - 1)
            for k in range(MT):
                pe.wait_ge(last_lo_ready, k + 1)
                last = products(acc[half][:, :], [(w_hi[2][:, w_slot, k, :], w_lo[2][:, w_slot, k, :],
                                                   h2_hi[:, slot, k, :], h2_lo[:, slot, k, :])], False, k == MT - 1)
            last.then_inc(l3_done, 1)
            pe.wait_ge(k_q_ready, 1)
            pe.wait_ge(first_mixed, 2)
            pe.wait_ge(warm_ready, 2)
            for h, c0, c1, n in OUT_ORDER:
                pe.wait_ge(cond_q_ready if h == 0 else piece_chain[n - 1], 1 if h == 0 else ROUNDED)
                pe.wait_ge(nan_ready[h], n)
                bank = y_bank[h, c0]
                for c in range((c1 - c0) // P):
                    cols = slice(c0 + c * P, c0 + (c + 1) * P)
                    pe.matmul(bank[:, c * P:(c + 1) * P], cond_q[:, h, cols], k_q[:, :], start=True, stop=False)
                    last = pe.matmul(bank[:, c * P:(c + 1) * P], nan_q[:, h, cols], zeros[:, :], start=False, stop=True)
                last.then_inc(y_ps[h], 1)


INPUTS = ["x", "cond_256", "L0_cond_rms_w", "L0_cond_wg_W", "L0_cond_wg_b", "L0_cond_gg_W", "L0_cond_gg_b",
          "L0_cond_W1", "L0_cond_b1", "L0_cond_W2", "L0_cond_b2", "L0_cond_W3", "L0_cond_b3",
          "L0_ffn_kernel", "L0_ffn_input_scale", "L0_ffn_kernel_scale", "L0_ffn_bias"]


def kernel(**inputs):
    import numpy as np
    import concourse.bacc as bacc
    from concourse.bass_utils import run_bass_kernel_spmd

    nc = bacc.Bacc("TRN2", target_bir_lowering=False, num_devices=1)
    arrays, args = {}, []
    for name in INPUTS:
        a = np.ascontiguousarray(inputs[name])
        arrays[f"in_{name}_dram"] = a
        args.append(nc.dram_tensor(f"in_{name}_dram", a.shape, mybir.dt.from_np(a.dtype), kind="ExternalInput").ap())
    args.append(nc.dram_tensor("out_0_dram", inputs["x"].shape, F32, kind="ExternalOutput").ap())
    adaln_ffn(nc, *args)
    r = run_bass_kernel_spmd(nc, [arrays], core_ids=[0])
    return r.results[0]["out_0_dram"]
```

```python
from contextlib import ExitStack

import concourse.bass as bass
from concourse import mybir
from concourse.alu_op_type import AluOpType as ALU

ACT = mybir.ActivationFunctionType
AX = mybir.AxisListType
F32 = mybir.dt.float32
F32R = mybir.dt.float32r
BF16 = mybir.dt.bfloat16
I32 = mybir.dt.int32

P = 128
WARM_UP = 6
EPS = 1e-6
EXPONENT_BITS = 0x7F800000
F8_LEAST_NORMAL = 2.0 ** -6
F8_ROUNDER = 1.5 * 2.0 ** 20
BF16_OVERFLOW = 7.319348e35


def adaln_ffn(nc, x, cond, rms_w, wg_W, wg_b, gg_W, gg_b, W1, b1, W2, b2, W3, b3,
              ffn_kernel, input_scale, kernel_scale, ffn_bias, out):
    B, S, H = x.shape
    E, _, M = W1.shape
    G = gg_W.shape[0]
    T = B * S // P
    HT = T // 2
    N = HT * P
    MT = M // P
    U = 2 * E
    PB = P // B
    assert (H, B, MT, N, G, E) == (P, 2, 2, 512, 32, 8)
    LOOP_FROM, LOOP_TURNS = 4, 2
    LOOP_END = LOOP_FROM + 4 * LOOP_TURNS

    x_tokens = x.rearrange("b (q t) h -> (b q) t h", t=T)
    out_tokens = out.rearrange("b (q t) h -> (b q) t h", t=T)

    TAIL = {U - 4: (E - 2, 0), U - 3: (E - 1, 0), U - 2: (E - 2, 1), U - 1: (E - 1, 1)}

    def place(u):
        expert, half = TAIL.get(u, (u // 2, u % 2))
        return expert, expert % 2, half, u % 2

    def loop_place(i, n):
        return i * 2 + n // 2, n // 2 % 2, n % 2, n % 2

    def wait(engine, sem, value):
        if not isinstance(value, int) or value > 0:
            engine.wait_ge(sem, value)

    with ExitStack() as ctx:
        def sb(name, shape, dt):
            return ctx.enter_context(nc.sbuf_tensor(name, shape, dt))

        def sem(name):
            return ctx.enter_context(nc.semaphore(name))

        x_tok = sb("x_tok", [P, T, H], F32)
        x_hi = sb("x_hi", [P, 2, N], F32R)
        x_lo = sb("x_lo", [P, 2, N], F32R)
        ident = sb("ident", [P, P], F32)
        w_raw = [sb("w1_raw", [P, 2, 1, M], F32), sb("w2_raw", [P, 2, MT, M], F32), sb("w3_raw", [P, 2, MT, H], F32)]
        w_hi = [sb("w1_hi", [P, 2, 1, M], F32R), sb("w2_hi", [P, 2, MT, M], F32R), sb("w3_hi", [P, 2, MT, H], F32R)]
        w_lo = [sb("w1_lo", [P, 2, 1, M], F32R), sb("w2_lo", [P, 2, MT, M], F32R), sb("w3_lo", [P, 2, MT, H], F32R)]
        bias_rows = sb("bias_rows", [2 * E * MT, P], F32)
        bias_cols = sb("bias_cols", [P, 2, E, MT], F32)
        bias_slot = sb("bias_slot", [P, 2, 2, MT], F32)
        b3_raw = sb("b3_raw", [3 * E, H], F32)
        b3_hi = sb("b3_hi", [3 * E, H], F32R)
        b3_lo = sb("b3_lo", [3 * E, H], F32R)
        h1 = sb("h1", [P, 2, MT, N], F32)
        h1_hi = sb("h1_hi", [P, 2, MT, N], F32R)
        h1_lo = sb("h1_lo", [P, 2, MT, N], F32R)
        h2 = sb("h2", [P, 2, MT, N], F32)
        h2_cw = sb("h2_cw", [P, MT, N], F32)
        h2_hi = sb("h2_hi", [P, 2, MT, N], F32R)
        h2_lo = sb("h2_lo", [P, 2, MT, N], F32R)
        warm = sb("warm", [P, N], BF16)
        x_sq = sb("x_sq", [P, T, H], F32)
        sum_sq = sb("sum_sq", [P, T], F32)
        var_eps = sb("var_eps", [P, T], F32)
        minus_half = sb("minus_half", [P, T], F32)
        inv_rms = sb("inv_rms", [P, T], F32)
        rms_col = sb("rms_col", [P, 1], F32)
        wg_raw = sb("wg_raw", [P, E], F32)
        wg_scaled = sb("wg_scaled", [P, E], F32)
        wg_hi = sb("wg_hi", [P, E], F32R)
        wg_lo = sb("wg_lo", [P, E], F32R)
        condT = sb("condT", [G, B], F32)
        genre_lhs = sb("genre_lhs", [G + 2, P], F32)
        genre_rhs = sb("genre_rhs", [G + 2, E], F32)
        gate_bias = sb("gate_bias", [P, E], F32)
        order = sb("order", [P, T, E], F32)
        logits = sb("logits", [P, T, E], F32)
        shifted = sb("shifted", [P, T, E], F32)
        top = sb("top", [P, T], F32)
        prob = sb("prob", [P, T, E], F32)
        prob_sum = sb("prob_sum", [P, T], F32)
        prob_inv = sb("prob_inv", [P, T], F32)
        second = sb("second", [P, T], F32)
        ties = sb("ties", [P, T, E], F32)
        first_of = sb("first_of", [P, T], F32)
        chosen1 = sb("chosen1", [P, T, E], F32)
        chosen2 = sb("chosen2", [P, T, E], F32)
        rest = sb("rest", [P, T, E], F32)
        cw_parts = sb("cw_parts", [P, T, 3 * E], F32)
        by_expert = sb("by_expert", [E, T * P], F32)
        mix_parts = sb("mix_parts", [3 * E, T * P], F32R)
        cw_row = sb("cw_row", [1, E, T * P], F32)
        cw_bc = sb("cw_bc", [P, E, T * P], F32)
        scales = sb("scales", [P, 2], F32)
        s_hi = sb("s_hi", [P, 2], F32R)
        s_lo = sb("s_lo", [P, 2], F32)
        inv = sb("inv", [P, 2], F32)
        inv_hi = sb("inv_hi", [P, 2], F32R)
        inv_rest = sb("inv_rest", [P, 2], F32)
        inv_part = sb("inv_part", [P, 2], F32)
        inv_err = sb("inv_err", [P, 2], F32)
        inv_lo = sb("inv_lo", [P, 2], F32)
        one = sb("one", [P, 2], F32)
        s_both = sb("s_both", [P, 1], F32)
        k_raw = sb("k_raw", [P, H], BF16)
        k_q = sb("k_q", [P, H], BF16)
        bias_bc = sb("bias_bc", [P, H], BF16)
        first_mix = sb("first_mix", [P, 2, N], F32)
        cond_out = sb("cond_out", [P, 2, N], BF16)
        zeros = sb("zeros", [P, H], BF16)
        q_a = sb("q_a", [P, 2, N], F32)
        q_v = sb("q_v", [P, 2, N], F32)
        q_m = sb("q_m", [P, 2, N], I32)
        q_r = sb("q_r", [P, 2, N], F32)
        q_s = sb("q_s", [P, 2, N], F32)
        cond_q = sb("cond_q", [P, 2, N], BF16)
        nan_q = sb("nan_q", [P, 2, N], BF16)
        k_a, k_v, k_r, k_s = (sb(n, [P, H], F32) for n in ("k_a", "k_v", "k_r", "k_s"))
        k_m = sb("k_m", [P, H], I32)
        k_nan = sb("k_nan", [P, H], BF16)
        y_bf = sb("y_bf", [P, 2, N], BF16)

        def bank(name):
            return ctx.enter_context(nc.psum_tensor(name, [P, N], F32))

        acc = [bank("acc0"), bank("acc1")]
        z1 = [bank("z1_0"), bank("z1_1")]
        z2 = [bank("z2_0"), bank("z2_1")]
        misc = [bank("misc0"), bank("misc1")]

        x_loaded = [sem("x_loaded0"), sem("x_loaded1")]
        w_loaded = [[sem(f"w{l + 1}_loaded{p}") for p in range(2)] for l in range(3)]
        gate_w_loaded = sem("gate_w_loaded")
        genre_loaded = sem("genre_loaded")
        bias_loaded = sem("bias_loaded")
        b3_zeroed = sem("b3_zeroed")
        b3_loaded = sem("b3_loaded")
        b3_hi_ready = sem("b3_hi_ready")
        b3_lo_ready = sem("b3_lo_ready")
        scales_loaded = sem("scales_loaded")
        kernel_loaded = sem("kernel_loaded")
        inv_ready = sem("inv_ready")
        pool_chain = sem("pool_chain")
        k_v_ready = sem("k_v_ready")
        k_chain = sem("k_chain")
        ffn_bias_loaded = sem("ffn_bias_loaded")
        warm_ready = sem("warm_ready")
        zeroed = sem("zeroed")
        ident_ready = sem("ident_ready")
        consts_ready = sem("consts_ready")
        genre_lhs_ready = sem("genre_lhs_ready")
        xT_ready = sem("xT_ready")
        x_hi_ready = sem("x_hi_ready")
        x_lo_ready = sem("x_lo_ready")
        x_sq_ready = sem("x_sq_ready")
        var_ready = sem("var_ready")
        inv_rms_ready = sem("inv_rms_ready")
        wg_split = sem("wg_split")
        gate_bias_ps = sem("gate_bias_ps")
        gate_bias_ready = sem("gate_bias_ready")
        bias_cols_ps = sem("bias_cols_ps")
        logitsT_ps = sem("logitsT_ps")
        logitsT_ready = sem("logitsT_ready")
        logits_ps = sem("logits_ps")
        shifted_ready = sem("shifted_ready")
        prob_ready = sem("prob_ready")
        cw_ready = sem("cw_ready")
        cwT_ps = sem("cwT_ps")
        cwT_ready = sem("cwT_ready")
        mix_parts_ready = sem("mix_parts_ready")
        cw_row_loaded = sem("cw_row_loaded")
        cw_bc_ready = sem("cw_bc_ready")
        w_hi_ready = [sem(f"w{l + 1}_hi_ready") for l in range(3)]
        w_lo_ready = [sem(f"w{l + 1}_lo_ready") for l in range(3)]
        bias_slot_ready = sem("bias_slot_ready")
        z1_ready = sem("z1_ready")
        z2_ready = sem("z2_ready")
        l3_done = sem("l3_done")
        h1_ready = sem("h1_ready")
        h1_hi_ready = sem("h1_hi_ready")
        h1_lo_ready = sem("h1_lo_ready")
        h2_ready = sem("h2_ready")
        h2_scaled = sem("h2_scaled")
        h2_hi_ready = sem("h2_hi_ready")
        h2_lo_ready = sem("h2_lo_ready")
        late_hi_ready = sem("late_hi_ready")
        late_lo_ready = sem("late_lo_ready")
        dve_chain = sem("dve_chain")
        k_q_ready = sem("k_q_ready")
        first_mixed = sem("first_mixed")
        pre_ready = sem("pre_ready")
        scales_ready = sem("scales_ready")
        cond_ready, qa_ready, qv_ready, qm_ready, qr_ready, qs_ready, cond_q_ready = (
            sem(n) for n in ("cond_ready", "qa_ready", "qv_ready", "qm_ready", "qr_ready", "qs_ready", "cond_q_ready"))
        piece_chain = [sem("piece_chain0"), sem("piece_chain1")]
        MIXED, QUOTIENT, ROUNDED = 2, 4, 8
        nan_ready = [sem("nan_ready0"), sem("nan_ready1")]
        y_ps = [sem("y_ps0"), sem("y_ps1")]
        y_bf_ready = [sem("y_bf_ready0"), sem("y_bf_ready1")]
        y_out_ready = [sem("y_out_ready0"), sem("y_out_ready1")]
        stored = sem("stored")

        CUT = 2 * P
        PIECES = ((0, 0, N, 1), (1, 0, CUT, 1), (1, CUT, N, 2))
        y_bank = {(0, 0): misc[0], (1, 0): z1[0], (1, CUT): z1[1]}

        def out_parts(h, c0, c1):
            t0, nt = h * HT + c0 // P, (c1 - c0) // P
            return (y_bf[:, h, c0:c1].rearrange("p (t f) -> p t f", f=H), x_tok[:, t0:t0 + nt, :],
                    bias_bc[:, :].unsqueeze(1).to_broadcast([P, nt, H]))

        block = ctx.enter_context(nc.Block())

        @block.sync
        def _(sp):
            def load_weights(l, expert, slot):
                W = (W1, W2, W3)[l]
                src = W[expert:expert + 1, :, :] if isinstance(expert, int) else W[bass.ds(expert, 1), :, :]
                sp.dma_start(w_raw[l][:, slot, :, :], src.rearrange("e (k p) n -> p (e k) n", p=P))\
                    .then_inc(w_loaded[l][slot], 16)

            sp.dma_start(x_tok[:, 0:HT, :], x_tokens[:, 0:HT, :]).then_inc(x_loaded[0], 16)
            load_weights(0, 0, 0)
            sp.dma_start(x_tok[:, HT:T, :], x_tokens[:, HT:T, :]).then_inc(x_loaded[1], 16)
            sp.dma_start(bias_rows[0:E * MT, :], b1.rearrange("e (m p) -> (e m) p", p=P)).then_inc(bias_loaded, 16)
            sp.dma_start(bias_rows[E * MT:2 * E * MT, :], b2.rearrange("e (m p) -> (e m) p", p=P)).then_inc(bias_loaded, 16)
            sp.dma_start(wg_raw[:, :], wg_W).then_inc(gate_w_loaded, 16)
            sp.dma_start(rms_col[:, :], rms_w.rearrange("(p o) -> p o", o=1)).then_inc(gate_w_loaded, 16)
            load_weights(1, 0, 0)
            sp.dma_start(scales[:, 0:1], input_scale.partition_broadcast(P)).then_inc(scales_loaded, 16)
            sp.dma_start(scales[:, 1:2], kernel_scale.partition_broadcast(P)).then_inc(scales_loaded, 16)
            load_weights(0, 1, 1)
            load_weights(1, 1, 1)
            load_weights(2, 0, 0)
            sp.dma_start(k_raw[:, :], ffn_kernel).then_inc(kernel_loaded, 16)
            load_weights(2, 1, 1)
            sp.wait_ge(b3_zeroed, 1)
            sp.dma_start(b3_raw[E:2 * E, :], b3).then_inc(b3_loaded, 16)
            sp.dma_start(b3_raw[2 * E:3 * E, :], b3).then_inc(b3_loaded, 16)
            sp.dma_start(bias_bc[:, :], ffn_bias.partition_broadcast(P)).then_inc(ffn_bias_loaded, 16)

            def reload_weights(expert, slot, layers=(0, 1, 2)):
                for l in layers:
                    sp.wait_ge(w_lo_ready[l], expert - 1)
                    load_weights(l, expert, slot)

            reload_weights(2, 0, (0, 1))
            reload_weights(3, 1, (0, 1))
            sp.wait_ge(cwT_ready, 2)
            sp.dma_start(cw_row[0:1, :, :], by_expert[0:E, :]).then_inc(cw_row_loaded, 16)
            reload_weights(2, 0, (2,))
            reload_weights(3, 1, (2,))
            with sp.Fori(0, (E - 4) // 2) as i:
                for slot in range(2):
                    reload_weights(i * 2 + (4 + slot), slot)
            for h, c0, c1, n in PIECES:
                t0, t1 = h * HT + c0 // P, h * HT + c1 // P
                sp.wait_ge(y_out_ready[h], n)
                sp.dma_start(out_tokens[:, t0:t1, :], x_tok[:, t0:t1, :]).then_inc(stored, 16)
            sp.wait_ge(stored, 16 * len(PIECES))

        @block.gpsimd
        def _(pool):
            pool.memset(ident[:, :], 0.0).then_inc(zeroed, 1)
            pool.wait_ge(zeroed, 1)
            pool.affine_select(out=ident[:, :], in_=ident[:, :], compare_op=ALU.not_equal, fill=1.0, base=0,
                               pattern=[[-1, P]], channel_multiplier=1).then_inc(ident_ready, 1)
            pool.memset(genre_lhs[:, :], 1.0).then_inc(consts_ready, 1)
            pool.memset(b3_raw[:, :], 0.0).then_inc(b3_zeroed, 1)
            pool.memset(minus_half[:, :], -0.5).then_inc(consts_ready, 1)
            for e in range(E):
                pool.memset(order[:, :, e:e + 1], float(E - e)).then_inc(consts_ready, 1)
            pool.dma_start(condT[:, :], cond.rearrange("b g -> g b"), allow_slow_non_contiguous=True).then_inc(genre_loaded, 16)
            pool.dma_start(genre_rhs[0:G, :], gg_W).then_inc(genre_loaded, 16)
            pool.dma_start(genre_rhs[G:G + 1, :], wg_b.rearrange("(o e) -> o e", o=1)).then_inc(genre_loaded, 16)
            pool.dma_start(genre_rhs[G + 1:G + 2, :], gg_b.rearrange("(o e) -> o e", o=1)).then_inc(genre_loaded, 16)

            def low_part(l, expert, slot):
                pool.wait_ge(w_hi_ready[l], expert + 1)
                pool.tensor_tensor(w_lo[l][:, slot, :, :], w_raw[l][:, slot, :, :],
                                   w_hi[l][:, slot, :, :].bitcast(F32), ALU.subtract).then_inc(w_lo_ready[l], 1)

            pool.wait_ge(x_loaded[1], 16)
            part = x_tok[:, HT:T, :]
            pool.tensor_tensor(x_sq[:, HT:T, :], part, part, ALU.mult).then_inc(x_sq_ready, 1)
            low_part(1, 0, 0)
            pool.wait_ge(consts_ready, 2)
            pool.wait_ge(var_ready, 1)
            pool.tensor_tensor(inv_rms[:, :], var_eps[:, :], minus_half[:, :], ALU.pow).then_inc(inv_rms_ready, 1)
            low_part(0, 1, 1)

            pool_count = [0]

            def link(instruction):
                pool_count[0] += 1
                instruction.then_inc(pool_chain, 1)
                pool.wait_ge(pool_chain, pool_count[0])

            pool.wait_ge(inv_ready, 1)
            pool.wait_ge(warm_ready, 3)
            link(pool.tensor_copy(s_hi[:, :], scales[:, :]))
            link(pool.tensor_copy(inv_hi[:, :], inv[:, :]))
            pool.tensor_tensor(s_lo[:, :], scales[:, :], s_hi[:, :].bitcast(F32), ALU.subtract)
            link(pool.tensor_tensor(inv_rest[:, :], inv[:, :], inv_hi[:, :].bitcast(F32), ALU.subtract))
            before = one[:, :]
            for a in (s_hi[:, :].bitcast(F32), s_lo[:, :]):
                for b in (inv_hi[:, :].bitcast(F32), inv_rest[:, :]):
                    link(pool.tensor_tensor(inv_part[:, :], a, b, ALU.mult))
                    link(pool.tensor_tensor(inv_err[:, :], before, inv_part[:, :], ALU.subtract))
                    before = inv_err[:, :]
            link(pool.tensor_tensor(inv_err[:, :], inv_err[:, :], inv[:, :], ALU.mult))
            pool.tensor_tensor(inv_lo[:, :], inv_rest[:, :], inv_err[:, :], ALU.add).then_inc(scales_ready, 1)
            pool.tensor_tensor(s_both[:, :], scales[:, 0:1], scales[:, 1:2], ALU.mult).then_inc(scales_ready, 1)

            low_part(1, 1, 1)
            low_part(2, 0, 0)
            pool.wait_ge(scales_ready, 1)
            pool.wait_ge(kernel_loaded, 16)
            link(pool.tensor_scalar(k_a[:, :], k_raw[:, :], inv_lo[:, 1:2], None, ALU.mult))
            link(pool.tensor_scalar(k_v[:, :], k_raw[:, :], inv_hi[:, 1:2].bitcast(F32), None, ALU.mult))
            pool.tensor_tensor(k_v[:, :], k_v[:, :], k_a[:, :], ALU.add).then_inc(k_v_ready, 1)
            pool.wait_ge(b3_loaded, 32)
            pool.tensor_copy(b3_hi[:, :], b3_raw[:, :]).then_inc(b3_hi_ready, 1)
            pool.wait_ge(b3_hi_ready, 1)
            pool.tensor_tensor(b3_lo[:, :], b3_raw[:, :], b3_hi[:, :].bitcast(F32), ALU.subtract).then_inc(b3_lo_ready, 1)
            low_part(0, 2, 0)

            def broadcast(e):
                pool.partition_broadcast(cw_bc[:, e, :], cw_row[0:1, e, :], P).then_inc(cw_bc_ready, 1)

            pool.wait_ge(cw_row_loaded, 16)
            broadcast(1)
            low_part(1, 2, 0)
            low_part(2, 1, 1)
            broadcast(0)
            low_part(0, 3, 1)
            broadcast(2)
            low_part(1, 3, 1)
            for e in range(3, E):
                broadcast(e)

            with pool.Fori(0, LOOP_TURNS) as i:
                for s in range(LOOP_FROM, LOOP_FROM + 4):
                    k, slot = i * 2 + s // 2, s // 2 % 2
                    if s % 2 == 0:
                        low_part(0, k + 2, slot)
                        low_part(2, k, slot)
                    else:
                        low_part(1, k + 2, slot)
            low_part(2, E - 2, 0)
            low_part(2, E - 1, 1)
            pool.wait_ge(qr_ready, 1)
            pool.tensor_tensor(q_s[:, 0, :], q_v[:, 0, :], q_r[:, 0, :], ALU.add).then_inc(qs_ready, 1)
            pool.wait_ge(qs_ready, 1)
            pool.tensor_tensor(cond_q[:, 0, :], q_s[:, 0, :], q_r[:, 0, :], ALU.subtract).then_inc(cond_q_ready, 1)
            pool.wait_ge(ffn_bias_loaded, 16)
            pool.wait_ge(y_bf_ready[0], 1)
            y_part, x_part, bias = out_parts(*PIECES[0][:3])
            link(pool.tensor_tensor(y_part, y_part, bias, ALU.add))
            pool.tensor_tensor(x_part, x_part, y_part, ALU.add).then_inc(y_out_ready[0], 1)

        @block.scalar
        def _(act):
            def high_part(l, expert, nth, slot):
                act.wait_ge(w_loaded[l][slot], nth * 16)
                if not isinstance(expert, int) or expert >= 2:
                    used, per_expert = ((z1_ready, 2 * MT), (z2_ready, 2 * MT), (l3_done, 2))[l]
                    act.wait_ge(used, (expert - 1) * per_expert)
                act.activation(w_hi[l][:, slot, :, :], w_raw[l][:, slot, :, :], ACT.Copy).then_inc(w_hi_ready[l], 1)

            def relu1(u, bias_count, at):
                _, w_slot, _, slot = at
                act.wait_ge(bias_slot_ready, bias_count)
                wait(act, h1_lo_ready, u - 1)
                for m in range(MT):
                    act.wait_ge(z1_ready, u * 2 + (m + 1))
                    act.activation(h1[:, slot, m, :], z1[m][:, :], ACT.Relu, bias=bias_slot[:, w_slot, 0, m:m + 1])\
                        .then_inc(h1_ready, 1)
                act.wait_ge(h1_ready, u * 2 + 2)
                wait(act, z2_ready, u * 2 - 2)
                act.activation(h1_hi[:, slot, :, :], h1[:, slot, :, :], ACT.Copy).then_inc(h1_hi_ready, 1)

            def relu2(u, at):
                _, w_slot, _, slot = at
                if isinstance(u, int) and u < 4:
                    wait(act, h2_lo_ready, u - 1)
                else:
                    act.wait_ge(h2_scaled, u - 3)
                for m in range(MT):
                    act.wait_ge(z2_ready, u * 2 + (m + 1))
                    act.activation(h2[:, slot, m, :], z2[m][:, :], ACT.Relu, bias=bias_slot[:, w_slot, 1, m:m + 1])\
                        .then_inc(h2_ready, 1)

            high_part(0, 0, 1, 0)
            for h in range(2):
                act.wait_ge(xT_ready, h + 1)
                act.activation(x_hi[:, h, :], misc[h][:, :], ACT.Copy).then_inc(x_hi_ready, 1)
            high_part(1, 0, 1, 0)
            relu1(0, 1, place(0))
            high_part(0, 1, 1, 1)

            def first_hi(u):
                act.wait_ge(h2_ready, u * 2 + 2)
                act.activation(h2_hi[:, u, :, :], h2[:, u, :, :], ACT.Copy).then_inc(h2_hi_ready, 1)

            relu1(1, 1, place(1))
            act.wait_ge(shifted_ready, 1)
            act.activation(prob[:, :, :], shifted[:, :, :], ACT.Exp).then_inc(prob_ready, 1)
            relu2(0, place(0))
            high_part(1, 1, 1, 1)
            first_hi(0)
            high_part(2, 0, 1, 0)
            relu1(2, 2, place(2))
            relu2(1, place(1))
            first_hi(1)
            relu1(3, 2, place(3))
            high_part(0, 2, 2, 0)
            for h in range(2):
                act.wait_ge(cwT_ready, h + 1)
                act.activation(mix_parts[:, h * N:(h + 1) * N], acc[h][0:3 * E, :], ACT.Copy).then_inc(mix_parts_ready, 1)
            high_part(2, 1, 1, 1)
            high_part(1, 2, 2, 0)
            relu2(2, place(2))
            high_part(0, 3, 2, 1)
            relu1(4, 3, place(4))
            relu2(3, place(3))
            high_part(1, 3, 2, 1)
            with act.Fori(0, LOOP_TURNS) as i:
                for s in range(LOOP_FROM, LOOP_FROM + 4):
                    relu1(i * 4 + (s + 1), i * 2 + ((s + 1) // 2 + 1), loop_place(i, s + 1))
                    relu2(i * 4 + s, loop_place(i, s))
                    k, slot = i * 2 + s // 2, s // 2 % 2
                    if s % 2 == 0:
                        high_part(0, k + 2, i + ((s // 2 + 2) // 2 + 1), slot)
                        high_part(2, k, i + (s // 2 // 2 + 1), slot)
                    else:
                        high_part(1, k + 2, i + ((s // 2 + 2) // 2 + 1), slot)
            for s in range(LOOP_END, U):
                if s + 1 < U:
                    relu1(s + 1, E, place(s + 1))
                    relu2(s, place(s))
                if s in (U - 4, U - 3):
                    expert = E - 2 + s - (U - 4)
                    high_part(2, expert, expert // 2 + 1, expert % 2)

            def nan_marks(h, c0, c1, n):
                act.wait_ge(qv_ready if h == 0 else piece_chain[n - 1], 1 if h == 0 else QUOTIENT)
                act.activation(nan_q[:, h, c0:c1], q_v[:, h, c0:c1], ACT.Copy, scale=BF16_OVERFLOW).then_inc(nan_ready[h], 1)

            _, _, _, slot = place(U - 2)
            act.wait_ge(l3_done, U - 3)
            for m in range(MT):
                act.wait_ge(h2_scaled, U - 3 + m)
                act.activation(h2_hi[:, slot, m, :], h2_cw[:, m, :], ACT.Copy).then_inc(late_hi_ready, 1)
            _, w_slot, _, slot = place(U - 1)
            act.wait_ge(h2_scaled, U - 4)
            act.wait_ge(l3_done, U - 2)
            act.wait_ge(scales_ready, 2)
            act.wait_ge(cond_ready, 1)
            act.activation(q_a[:, 0, :], cond_out[:, 0, :], ACT.Copy, scale=inv_lo[:, 0:1]).then_inc(qa_ready, 1)
            for m in range(MT):
                act.wait_ge(z2_ready, (U - 1) * MT + m + 1)
                bias = bias_slot[:, w_slot, 1, m:m + 1]
                act.activation(h2_hi[:, slot, m, :], z2[m][:, :], ACT.Relu, bias=bias).then_inc(late_hi_ready, 1)
                act.activation(h2[:, slot, m, :], z2[m][:, :], ACT.Relu, bias=bias).then_inc(h2_ready, 1)
            nan_marks(*PIECES[0])
            for h, c0, c1, n in PIECES[1:]:
                act.wait_ge(piece_chain[n - 1], MIXED)
                act.activation(q_a[:, h, c0:c1], cond_out[:, h, c0:c1], ACT.Copy, scale=inv_lo[:, 0:1])\
                    .then_inc(piece_chain[n - 1], 1)
            for piece in PIECES[1:]:
                nan_marks(*piece)
            for h, c0, c1, n in PIECES:
                act.wait_ge(y_ps[h], n)
                act.activation(y_bf[:, h, c0:c1], y_bank[h, c0][:, 0:c1 - c0], ACT.Copy, scale=s_both[:, 0:1])\
                    .then_inc(y_bf_ready[h], 1)

        @block.vector
        def _(dve):
            count = [0]

            def link(instruction):
                count[0] += 1
                instruction.then_inc(dve_chain, 1)
                dve.wait_ge(dve_chain, count[0])

            def per_token(v):
                return v[:, :].unsqueeze(2).to_broadcast([P, T, E])

            def x_low(h):
                dve.wait_ge(x_hi_ready, h + 1)
                dve.tensor_tensor(x_lo[:, h, :], misc[h][:, :], x_hi[:, h, :].bitcast(F32), ALU.subtract)\
                    .then_inc(x_lo_ready, 1)

            dve.memset(warm[:, :], 0.0).then_inc(warm_ready, 1)
            dve.memset(zeros[:, :], 0.0).then_inc(warm_ready, 1)
            dve.memset(one[:, :], 1.0).then_inc(warm_ready, 1)
            dve.wait_ge(x_loaded[0], 16)
            link(dve.tensor_tensor(x_sq[:, 0:HT, :], x_tok[:, 0:HT, :], x_tok[:, 0:HT, :], ALU.mult))
            dve.wait_ge(w_hi_ready[0], 1)
            dve.tensor_tensor(w_lo[0][:, 0, :, :], w_raw[0][:, 0, :, :], w_hi[0][:, 0, :, :].bitcast(F32),
                              ALU.subtract).then_inc(w_lo_ready[0], 1)
            x_low(0)
            dve.wait_ge(gate_w_loaded, 32)
            link(dve.tensor_scalar(wg_scaled[:, :], wg_raw[:, :], rms_col[:, 0:1], None, ALU.mult))
            link(dve.tensor_copy(wg_hi[:, :], wg_scaled[:, :]))
            dve.tensor_tensor(wg_lo[:, :], wg_scaled[:, :], wg_hi[:, :].bitcast(F32), ALU.subtract).then_inc(wg_split, 1)
            x_low(1)
            dve.wait_ge(bias_cols_ps, 1)
            link(dve.tensor_copy(bias_cols[:, :, :, :].rearrange("p l e m -> p (l e m)"), z2[0][:, 0:2 * E * MT]))

            def load_bias_slot(expert, slot):
                src = bias_cols[:, :, expert:expert + 1, :] if isinstance(expert, int) else bias_cols[:, :, bass.ds(expert, 1), :]
                dve.tensor_scalar(bias_slot[:, slot, :, :], src.rearrange("p l o m -> p l (o m)"), 1.0, None, ALU.mult)\
                    .then_inc(bias_slot_ready, 1)

            load_bias_slot(0, 0)
            dve.wait_ge(x_sq_ready, 1)
            dve.reduce_sum(sum_sq[:, 0:HT], x_sq[:, 0:HT, :], AX.X)
            link(dve.reduce_sum(sum_sq[:, HT:T], x_sq[:, HT:T, :], AX.X))
            dve.tensor_scalar(var_eps[:, :], sum_sq[:, :], 1.0 / H, EPS, ALU.mult, ALU.add).then_inc(var_ready, 1)
            dve.wait_ge(consts_ready, 2)
            dve.wait_ge(genre_loaded, 64)
            for b in range(B):
                dve.tensor_copy(genre_lhs[0:G, b * PB:(b + 1) * PB], condT[:, b:b + 1].to_broadcast([G, PB]))\
                    .then_inc(genre_lhs_ready, 1)
            load_bias_slot(1, 1)

            def h1_low(u, at):
                slot = at[3]
                dve.wait_ge(h1_hi_ready, u + 1)
                dve.tensor_tensor(h1_lo[:, slot, :, :], h1[:, slot, :, :], h1_hi[:, slot, :, :].bitcast(F32),
                                  ALU.subtract).then_inc(h1_lo_ready, 1)

            for h in range(2):
                dve.wait_ge(logitsT_ps, h + 1)
                dve.tensor_copy(by_expert[0:E, h * N:(h + 1) * N], acc[h][0:E, :]).then_inc(logitsT_ready, 1)
            h1_low(0, place(0))
            dve.wait_ge(scales_loaded, 32)
            dve.reciprocal(inv[:, :], scales[:, :]).then_inc(inv_ready, 1)
            dve.wait_ge(gate_bias_ps, 1)
            dve.tensor_copy(gate_bias[:, :], misc[1][:, 0:E]).then_inc(gate_bias_ready, 1)
            dve.wait_ge(inv_rms_ready, 1)
            dve.wait_ge(logits_ps, 1)
            link(dve.tensor_tensor(logits[:, :, :], misc[0][:, 0:T * E].rearrange("p (t e) -> p t e", e=E),
                                   per_token(inv_rms), ALU.mult))
            dve.wait_ge(gate_bias_ready, 1)
            link(dve.tensor_tensor(logits[:, :, :], logits[:, :, :],
                                   gate_bias[:, :].unsqueeze(1).to_broadcast([P, T, E]), ALU.add))
            link(dve.reduce_max(top[:, :], logits[:, :, :], AX.X))
            dve.tensor_tensor(shifted[:, :, :], logits[:, :, :], per_token(top), ALU.subtract).then_inc(shifted_ready, 1)
            dve.wait_ge(consts_ready, 2 + E)

            def choose(of, largest, chosen):
                link(dve.tensor_tensor(ties[:, :, :], of[:, :, :], per_token(largest), ALU.is_equal))
                link(dve.tensor_tensor(ties[:, :, :], ties[:, :, :], order[:, :, :], ALU.mult))
                link(dve.reduce_max(first_of[:, :], ties[:, :, :], AX.X))
                link(dve.tensor_tensor(chosen[:, :, :], ties[:, :, :], per_token(first_of), ALU.is_equal))

            choose(logits, top, chosen1)
            link(dve.scalar_tensor_tensor(rest[:, :, :], chosen1[:, :, :], -3.0e38, logits[:, :, :], ALU.mult, ALU.add))
            link(dve.reduce_max(second[:, :], rest[:, :, :], AX.X))
            h1_low(1, place(1))
            choose(rest, second, chosen2)
            link(dve.tensor_tensor(chosen1[:, :, :], chosen1[:, :, :], chosen2[:, :, :], ALU.add))
            dve.wait_ge(prob_ready, 1)
            link(dve.reduce_sum(prob_sum[:, :], prob[:, :, :], AX.X))
            cw, cw_hi, cw_lo = (cw_parts[:, :, n * E:(n + 1) * E] for n in range(3))
            dve.tensor_tensor(cw, prob[:, :, :], chosen1[:, :, :], ALU.mult)
            link(dve.reciprocal(prob_inv[:, :], prob_sum[:, :]))
            link(dve.tensor_tensor(cw, cw, per_token(prob_inv), ALU.mult))
            link(dve.tensor_copy(cw_hi.bitcast(F32R), cw))
            dve.tensor_tensor(cw_lo, cw, cw_hi, ALU.subtract).then_inc(cw_ready, 1)

            def first_low(u):
                dve.wait_ge(h2_hi_ready, u + 1)
                dve.tensor_tensor(h2_lo[:, u, :, :], h2[:, u, :, :], h2_hi[:, u, :, :].bitcast(F32), ALU.subtract)\
                    .then_inc(h2_lo_ready, 1)

            first_low(0)
            h1_low(2, place(2))
            for h in range(2):
                dve.wait_ge(cwT_ps, h + 1)
                dve.tensor_copy(by_expert[:, h * N:(h + 1) * N], acc[h][0:E, :]).then_inc(cwT_ready, 1)

            def split_h2(u, at):
                expert, _, half, slot = at
                dve.wait_ge(h2_ready, u * 2 + 2)
                dve.wait_ge(cw_bc_ready, 1 if isinstance(expert, int) and expert == 1 else expert + 1)
                which = slice(expert, expert + 1) if isinstance(expert, int) else bass.ds(expert, 1)
                mix = cw_bc[:, which, half * N:(half + 1) * N].to_broadcast([P, MT, N])
                dve.wait_ge(h2_lo_ready, u)
                dve.tensor_tensor(h2_cw[:, :, :], h2[:, slot, :, :], mix, ALU.mult).then_inc(h2_scaled, 1)
                dve.wait_ge(h2_scaled, u - 1)
                dve.wait_ge(l3_done, u - 1)
                dve.tensor_copy(h2_hi[:, slot, :, :], h2_cw[:, :, :]).then_inc(h2_hi_ready, 1)
                dve.wait_ge(h2_hi_ready, u + 1)
                dve.tensor_tensor(h2_lo[:, slot, :, :], h2_cw[:, :, :], h2_hi[:, slot, :, :].bitcast(F32),
                                  ALU.subtract).then_inc(h2_lo_ready, 1)

            def mix_first(h):
                dve.wait_ge(l3_done, h + 1)
                dve.wait_ge(cw_bc_ready, 2)
                dve.tensor_tensor(first_mix[:, h, :], misc[h][:, :], cw_bc[:, 0, h * N:(h + 1) * N], ALU.mult)\
                    .then_inc(first_mixed, 1)

            def quotient(a, v_lo, v, c):
                return dve.scalar_tensor_tensor(v, a, inv_hi[:, c:c + 1].bitcast(F32), v_lo, ALU.mult, ALU.add)

            def exponent(v, m):
                return dve.tensor_scalar(m, v.bitcast(I32), EXPONENT_BITS, None, ALU.bitwise_and)

            def rounder(m, r):
                return dve.tensor_scalar(r, m.bitcast(F32), F8_LEAST_NORMAL, F8_ROUNDER, ALU.max, ALU.mult)

            def biases_due(k, slot):
                dve.wait_ge(h2_ready, k * 4)
                load_bias_slot(k + 1, slot)

            biases_due(1, 0)
            first_low(1)
            dve.wait_ge(k_v_ready, 1)
            dve.tensor_scalar(k_nan[:, :], k_v[:, :], BF16_OVERFLOW, None, ALU.mult).then_inc(k_chain, 1)
            exponent(k_v[:, :], k_m[:, :]).then_inc(k_chain, 1)
            dve.wait_ge(k_chain, 1)
            dve.tensor_scalar(k_nan[:, :], k_nan[:, :], 0.0, None, ALU.mult).then_inc(k_chain, 1)
            dve.wait_ge(k_chain, 2)
            rounder(k_m[:, :], k_r[:, :]).then_inc(k_chain, 1)
            dve.wait_ge(k_chain, 4)
            dve.tensor_tensor(k_s[:, :], k_v[:, :], k_r[:, :], ALU.add).then_inc(k_chain, 1)
            dve.wait_ge(k_chain, 5)
            dve.tensor_tensor(k_a[:, :], k_s[:, :], k_r[:, :], ALU.subtract).then_inc(k_chain, 1)
            dve.wait_ge(k_chain, 6)
            dve.tensor_tensor(k_q[:, :], k_a[:, :], k_nan[:, :], ALU.add).then_inc(k_q_ready, 1)
            h1_low(3, place(3))
            split_h2(2, place(2))
            h1_low(4, place(4))
            mix_first(0)
            with dve.Fori(0, LOOP_TURNS) as i:
                for s in range(LOOP_FROM, LOOP_FROM + 4):
                    if s % 2 == 0:
                        biases_due(i * 2 + s // 2, (s // 2 + 1) % 2)
                    split_h2(i * 4 + (s - 1), loop_place(i, s - 1))
                    h1_low(i * 4 + (s + 1), loop_place(i, s + 1))
            biases_due(E - 2, 1)
            split_h2(LOOP_END - 1, place(LOOP_END - 1))
            h1_low(LOOP_END + 1, place(LOOP_END + 1))
            mix_first(1)
            split_h2(LOOP_END, place(LOOP_END))
            h1_low(LOOP_END + 2, place(LOOP_END + 2))
            split_h2(LOOP_END + 1, place(LOOP_END + 1))
            h1_low(LOOP_END + 3, place(LOOP_END + 3))
            u = U - 2
            expert, _, half, slot = place(u)
            dve.wait_ge(h2_lo_ready, u)
            for m in range(MT):
                dve.wait_ge(h2_ready, u * 2 + m + 1)
                dve.tensor_tensor(h2_cw[:, m, :], h2[:, slot, m, :], cw_bc[:, expert, half * N:(half + 1) * N],
                                  ALU.mult).then_inc(h2_scaled, 1)
            dve.wait_ge(l3_done, U - 2)
            dve.wait_ge(first_mixed, 2)
            dve.tensor_tensor(cond_out[:, 0, :], acc[0][:, :], first_mix[:, 0, :], ALU.add).then_inc(cond_ready, 1)
            dve.wait_ge(h2_scaled, u)
            dve.wait_ge(l3_done, u - 1)
            for m in range(MT):
                dve.wait_ge(late_hi_ready, m + 1)
                dve.tensor_tensor(h2_lo[:, slot, m, :], h2_cw[:, m, :], h2_hi[:, slot, m, :].bitcast(F32),
                                  ALU.subtract).then_inc(late_lo_ready, 1)

            def last_low(m):
                slot = place(U - 1)[3]
                dve.wait_ge(h2_ready, (U - 1) * 2 + m + 1)
                dve.wait_ge(late_hi_ready, MT + m + 1)
                dve.tensor_tensor(h2_lo[:, slot, m, :], h2[:, slot, m, :], h2_hi[:, slot, m, :].bitcast(F32),
                                  ALU.subtract).then_inc(late_lo_ready, 1)

            dve.wait_ge(scales_ready, 1)
            dve.wait_ge(cond_ready, 1)
            dve.wait_ge(qa_ready, 1)
            quotient(cond_out[:, 0, :], q_a[:, 0, :], q_v[:, 0, :], 0).then_inc(qv_ready, 1)
            dve.wait_ge(qv_ready, 1)
            exponent(q_v[:, 0, :], q_m[:, 0, :]).then_inc(qm_ready, 1)
            last_low(0)
            dve.wait_ge(qm_ready, 1)
            rounder(q_m[:, 0, :], q_r[:, 0, :]).then_inc(qr_ready, 1)
            last_low(1)
            dve.wait_ge(l3_done, U - 1)
            dve.tensor_tensor(first_mix[:, 1, :], acc[1][:, :], first_mix[:, 1, :], ALU.add).then_inc(pre_ready, 1)

            ends = PIECES[1:]
            done = [0] * len(ends)

            def by_turns(stage):
                for n, (_, c0, c1, _) in enumerate(ends):
                    if done[n]:
                        dve.wait_ge(piece_chain[n], done[n])
                    stage(slice(c0, c1)).then_inc(piece_chain[n], 1)
                    done[n] += 1

            dve.wait_ge(l3_done, U)
            dve.wait_ge(pre_ready, 1)
            last_mix = cw_bc[:, E - 1, N:2 * N]
            by_turns(lambda c: dve.tensor_tensor(q_a[:, 1, c], misc[1][:, c], last_mix[:, c], ALU.mult))
            by_turns(lambda c: dve.tensor_tensor(cond_out[:, 1, c], q_a[:, 1, c], first_mix[:, 1, c], ALU.add))
            for n in range(len(ends)):
                done[n] += 1
            by_turns(lambda c: quotient(cond_out[:, 1, c], q_a[:, 1, c], q_v[:, 1, c], 0))
            by_turns(lambda c: exponent(q_v[:, 1, c], q_m[:, 1, c]))
            by_turns(lambda c: rounder(q_m[:, 1, c], q_r[:, 1, c]))
            by_turns(lambda c: dve.tensor_tensor(q_s[:, 1, c], q_v[:, 1, c], q_r[:, 1, c], ALU.add))
            by_turns(lambda c: dve.tensor_tensor(cond_q[:, 1, c], q_s[:, 1, c], q_r[:, 1, c], ALU.subtract))
            dve.wait_ge(ffn_bias_loaded, 16)
            for h, c0, c1, n in PIECES[1:]:
                y_part, x_part, bias = out_parts(h, c0, c1)
                dve.wait_ge(y_bf_ready[h], n)
                link(dve.tensor_tensor(y_part, y_part, bias, ALU.add))
                dve.tensor_tensor(x_part, x_part, y_part, ALU.add).then_inc(y_out_ready[h], 1)

        @block.tensor
        def _(pe):
            pe.wait_ge(warm_ready, 1)
            for _ in range(WARM_UP):
                pe.matmul(z1[1][:, :], warm[:, 0:P], warm[:, :], start=True, stop=True)
            pe.wait_ge(ident_ready, 1)

            def transpose_x(h):
                pe.wait_ge(x_loaded[h], 16)
                for c in range(HT):
                    last = pe.transpose(misc[h][:, c * P:(c + 1) * P], x_tok[:, h * HT + c, :], ident[:, :])
                last.then_inc(xT_ready, 1)

            def products(bank, parts, start, stop, lo_sem=None, lo_count=0):
                n, passes = 0, 3 * len(parts)
                for wh, wl, mh, ml in parts:
                    for a, b in ((wh, mh), (wl, mh), (wh, ml)):
                        if lo_sem is not None and n == 2:
                            pe.wait_ge(lo_sem, lo_count)
                        last = pe.matmul(bank, a, b, start=start and n == 0, stop=stop and n == passes - 1)
                        n += 1
                return last

            def layer1(u, at, new_expert, lo_sem=None, lo_count=0):
                expert, w_slot, half, _ = at
                if new_expert:
                    pe.wait_ge(w_lo_ready[0], expert + 1)
                for m in range(MT):
                    wait(pe, h1_ready, u * 2 + (m - 1))
                    cols = slice(m * P, (m + 1) * P)
                    products(z1[m][:, :], [(w_hi[0][:, w_slot, 0, cols], w_lo[0][:, w_slot, 0, cols],
                                            x_hi[:, half, :], x_lo[:, half, :])], True, True, lo_sem, lo_count)\
                        .then_inc(z1_ready, 1)

            def layer2(u, at, new_expert):
                expert, w_slot, _, slot = at
                if new_expert:
                    pe.wait_ge(w_lo_ready[1], expert + 1)
                pe.wait_ge(h1_lo_ready, u + 1)
                for m in range(MT):
                    wait(pe, h2_ready, u * 2 + (m - 1))
                    cols = slice(m * P, (m + 1) * P)
                    products(z2[m][:, :], [(w_hi[1][:, w_slot, k, cols], w_lo[1][:, w_slot, k, cols],
                                            h1_hi[:, slot, k, :], h1_lo[:, slot, k, :]) for k in range(MT)],
                             True, True).then_inc(z2_ready, 1)

            def early_layer2(u, at, new_expert):
                expert, w_slot, _, slot = at
                if new_expert:
                    pe.wait_ge(w_lo_ready[1], expert + 1)
                pe.wait_ge(h1_hi_ready, u + 1)
                for m in range(MT):
                    wait(pe, h2_ready, u * 2 + (m - 1))
                    cols = slice(m * P, (m + 1) * P)
                    for k in range(MT):
                        pe.matmul(z2[m][:, :], w_hi[1][:, w_slot, k, cols], h1_hi[:, slot, k, :], start=k == 0, stop=False)
                        pe.matmul(z2[m][:, :], w_lo[1][:, w_slot, k, cols], h1_hi[:, slot, k, :], start=False, stop=False)
                pe.wait_ge(h1_lo_ready, u + 1)
                for m in range(MT):
                    cols = slice(m * P, (m + 1) * P)
                    for k in range(MT):
                        last = pe.matmul(z2[m][:, :], w_hi[1][:, w_slot, k, cols], h1_lo[:, slot, k, :],
                                         start=False, stop=k == MT - 1)
                    last.then_inc(z2_ready, 1)

            def layer3(u, at, new_expert, stop=False):
                expert, w_slot, half, slot = at
                first = isinstance(expert, int) and expert == 0
                if new_expert:
                    pe.wait_ge(w_lo_ready[2], expert + 1)
                pe.wait_ge(h2_lo_ready, u + 1)
                products((misc if first else acc)[half][:, :],
                         [(w_hi[2][:, w_slot, k, :], w_lo[2][:, w_slot, k, :],
                           h2_hi[:, slot, k, :], h2_lo[:, slot, k, :]) for k in range(MT)],
                         first, first or stop).then_inc(l3_done, 1)

            transpose_x(0)
            transpose_x(1)
            pe.wait_ge(bias_loaded, 32)
            nb = 2 * E * MT
            pe.transpose(z2[0][:, 0:nb], bias_rows[:, :], ident[0:nb, 0:nb]).then_inc(bias_cols_ps, 1)
            pe.wait_ge(x_hi_ready, 1)
            layer1(0, place(0), True, x_lo_ready, 1)
            pe.wait_ge(wg_split, 1)
            for h in range(2):
                pe.wait_ge(x_lo_ready, h + 1)
                products(acc[h][0:E, :], [(wg_hi[:, :], wg_lo[:, :], x_hi[:, h, :], x_lo[:, h, :])], True, True)\
                    .then_inc(logitsT_ps, 1)
            layer1(1, place(1), False)
            pe.wait_ge(genre_lhs_ready, 2)
            pe.matmul(misc[1][:, 0:E], genre_lhs[:, :], genre_rhs[:, :], start=True, stop=True).then_inc(gate_bias_ps, 1)
            pe.wait_ge(logitsT_ready, 2)
            for c in range(T):
                last = pe.transpose(misc[0][:, c * E:(c + 1) * E], by_expert[0:E, c * P:(c + 1) * P], ident[0:E, 0:E])
            last.then_inc(logits_ps, 1)
            pe.wait_ge(bias_slot_ready, 1)
            early_layer2(0, place(0), True)
            layer1(2, place(2), True)
            early_layer2(1, place(1), False)
            for s in range(2, LOOP_FROM):
                layer1(s + 1, place(s + 1), s % 2 == 1)
                if s == 2:
                    pe.wait_ge(cw_ready, 1)
                    for h in range(2):
                        for c in range(HT):
                            last = pe.transpose(acc[h][0:3 * E, c * P:(c + 1) * P], cw_parts[:, h * HT + c, :], ident[:, :])
                        last.then_inc(cwT_ps, 1)
                    layer3(0, place(0), True)
                layer2(s, place(s), s % 2 == 0)
                if s == 3:
                    pe.wait_ge(b3_lo_ready, 1)
                    pe.wait_ge(cwT_ready, 2)
                    pe.wait_ge(mix_parts_ready, 2)
                    for h in range(2):
                        mix = mix_parts[:, h * N:(h + 1) * N]
                        pe.matmul(acc[h][:, :], b3_hi[:, :], mix, start=True, stop=False)
                        pe.matmul(acc[h][:, :], b3_lo[:, :], mix, start=False, stop=False)
                layer3(s - 1, place(s - 1), s % 2 == 1)
            with pe.Fori(0, LOOP_TURNS) as i:
                for s in range(LOOP_FROM, LOOP_FROM + 4):
                    layer1(i * 4 + (s + 1), loop_place(i, s + 1), s % 2 == 1)
                    layer2(i * 4 + s, loop_place(i, s), s % 2 == 0)
                    layer3(i * 4 + (s - 1), loop_place(i, s - 1), s % 2 == 1)
            for s in range(LOOP_END, U):
                if s + 1 < U:
                    layer1(s + 1, place(s + 1), s == LOOP_END)
                layer2(s, place(s), s in (LOOP_END, LOOP_END + 1))
                if s - 1 < U - 2:
                    layer3(s - 1, place(s - 1), s in (LOOP_END + 1, LOOP_END + 2), stop=s - 1 == U - 3)
            _, w_slot, half, slot = place(U - 2)
            for k in range(MT):
                pe.wait_ge(late_lo_ready, k + 1)
                last = products(acc[half][:, :], [(w_hi[2][:, w_slot, k, :], w_lo[2][:, w_slot, k, :],
                                                   h2_hi[:, slot, k, :], h2_lo[:, slot, k, :])], False, k == MT - 1)
            last.then_inc(l3_done, 1)
            _, w_slot, half, slot = place(U - 1)
            pe.wait_ge(first_mixed, 2)
            for k in range(MT):
                pe.wait_ge(late_hi_ready, MT + k + 1)
                pe.matmul(misc[half][:, :], w_hi[2][:, w_slot, k, :], h2_hi[:, slot, k, :], start=k == 0, stop=False)
                pe.matmul(misc[half][:, :], w_lo[2][:, w_slot, k, :], h2_hi[:, slot, k, :], start=False, stop=False)
                pe.wait_ge(late_lo_ready, MT + k + 1)
                last = pe.matmul(misc[half][:, :], w_hi[2][:, w_slot, k, :], h2_lo[:, slot, k, :],
                                 start=False, stop=k == MT - 1)
            last.then_inc(l3_done, 1)
            pe.wait_ge(k_q_ready, 1)
            pe.wait_ge(warm_ready, 2)
            for h, c0, c1, n in PIECES:
                pe.wait_ge(nan_ready[h], n)
                for c in range((c1 - c0) // P):
                    cols = slice(c0 + c * P, c0 + (c + 1) * P)
                    y_cols = y_bank[h, c0][:, c * P:(c + 1) * P]
                    pe.matmul(y_cols, nan_q[:, h, cols], zeros[:, :], start=True, stop=False)
                    if c == 0:
                        pe.wait_ge(cond_q_ready if h == 0 else piece_chain[n - 1], 1 if h == 0 else ROUNDED)
                    last = pe.matmul(y_cols, cond_q[:, h, cols], k_q[:, :], start=False, stop=True)
                last.then_inc(y_ps[h], 1)


INPUTS = ["x", "cond_256", "L0_cond_rms_w", "L0_cond_wg_W", "L0_cond_wg_b", "L0_cond_gg_W", "L0_cond_gg_b",
          "L0_cond_W1", "L0_cond_b1", "L0_cond_W2", "L0_cond_b2", "L0_cond_W3", "L0_cond_b3",
          "L0_ffn_kernel", "L0_ffn_input_scale", "L0_ffn_kernel_scale", "L0_ffn_bias"]


def kernel(**inputs):
    import numpy as np
    import concourse.bacc as bacc
    from concourse.bass_utils import run_bass_kernel_spmd

    nc = bacc.Bacc("TRN2", target_bir_lowering=False, num_devices=1)
    arrays, args = {}, []
    for name in INPUTS:
        a = np.ascontiguousarray(inputs[name])
        arrays[f"in_{name}_dram"] = a
        args.append(nc.dram_tensor(f"in_{name}_dram", a.shape, mybir.dt.from_np(a.dtype), kind="ExternalInput").ap())
    args.append(nc.dram_tensor("out_0_dram", inputs["x"].shape, F32, kind="ExternalOutput").ap())
    adaln_ffn(nc, *args)
    r = run_bass_kernel_spmd(nc, [arrays], core_ids=[0])
    return r.results[0]["out_0_dram"]
```
